# Optimizing a Trainium2 kernel written in Bass

```python
import numpy as np
import jax
import jax.numpy as jnp

def _softmax(x, axis=-1):
    return jax.nn.softmax(x, axis=axis)

def _gelu(x):
    return jax.nn.gelu(x, approximate=True)

def _silu(x):
    return jax.nn.silu(x)

def _sigmoid(x):
    return jax.nn.sigmoid(x)

def _layernorm(x, axis=-1, eps=1e-05):
    m = jnp.mean(x, axis=axis, keepdims=True)
    v = jnp.var(x, axis=axis, keepdims=True)
    return (x - m) / jnp.sqrt(v + eps)

def _scatter_add(tgt, idx, src, axis=0):
    return tgt.at[idx].add(src)

def _segment_sum(src, seg, n):
    return jax.ops.segment_sum(src, seg, n)
kernel_name = 'mk_adj_ffn_d1_adj_r2_6334aa'

def setup_inputs(seed: int=0):
    np.random.seed(seed)
    _w = jnp.asarray

    def _rec_inputs():
        import jax
        import jax.numpy as jnp
        _gk = jax.random.key(seed)
        x = -0.0002422 + 1 * jax.random.normal(jax.random.fold_in(_gk, 1), (32, 256, 512), jnp.float32)
        _w = (1.0 + jnp.arange(256, dtype=jnp.float32)) ** (-0.5)
        _w = _w / _w.mean()
        _pij = jnp.clip(0.03125 * _w[:, None] * _w[None, :], 0.0, 1.0)
        _a = jax.random.uniform(jax.random.fold_in(_gk, 2), (32, 256, 256)) < _pij
        adj = _a.astype(jnp.int32)
        return (x, adj)
    x, adj = _rec_inputs()

    def _L0_gnn_setup():
        import jax, jax.numpy as jnp
        import numpy as np
        IN_DIM = 512
        OUT_DIM = 512
        BATCH = 128
        NUM_OBJS = 100
        key = jax.random.key(seed)
        k1, k2, k3, k4, k5 = jax.random.split(key, 5)
        stdv = 1.0 / np.sqrt(OUT_DIM)
        feature = jax.random.normal(k1, (BATCH, NUM_OBJS, IN_DIM), dtype=jnp.float32)
        graph = jax.random.randint(k2, (BATCH, NUM_OBJS, NUM_OBJS), 0, 2, dtype=jnp.int32)
        weight = jax.random.uniform(k3, (IN_DIM, OUT_DIM), dtype=jnp.float32, minval=-stdv, maxval=stdv)
        wq = jax.random.uniform(k4, (IN_DIM, OUT_DIM), dtype=jnp.float32, minval=-stdv, maxval=stdv)
        wk = jax.random.uniform(k5, (IN_DIM, OUT_DIM), dtype=jnp.float32, minval=-stdv, maxval=stdv)
        return {'feature': feature, 'graph': graph, 'weight': weight, 'wq': wq, 'wk': wk}
    _L0_gnn_all = _L0_gnn_setup()
    _L0_gnn_in = {k: v for k, v in _L0_gnn_all.items() if k in ('weight', 'wq', 'wk')}
    del _L0_gnn_all

    def _L0_ffn_setup():
        import jax, jax.numpy as jnp
        import numpy as np
        CAPACITY_FACTOR = 0.5
        NUM_HEADS = 16
        key = jax.random.key(seed)
        ks = jax.random.split(key, 6)
        B, N, D = (4, 2048, 512)
        s = 1.0 / np.sqrt(D)
        return {'token_inputs': jax.random.normal(ks[0], (B, N, D), jnp.float32), 'Wg': jax.random.normal(ks[1], (D, 1), jnp.float32) * s, 'Wq': jax.random.normal(ks[2], (D, D), jnp.float32) * s, 'Wk': jax.random.normal(ks[3], (D, D), jnp.float32) * s, 'Wv': jax.random.normal(ks[4], (D, D), jnp.float32) * s, 'Wo': jax.random.normal(ks[5], (D, D), jnp.float32) * s}
    _L0_ffn_all = _L0_ffn_setup()
    _L0_ffn_in = {k: v for k, v in _L0_ffn_all.items() if k in ('Wg', 'Wq', 'Wk', 'Wv', 'Wo')}
    del _L0_ffn_all
    return {'x': x, 'adj': adj, 'L0_gnn_weight': _L0_gnn_in['weight'], 'L0_gnn_wq': _L0_gnn_in['wq'], 'L0_gnn_wk': _L0_gnn_in['wk'], 'L0_ffn_Wg': _L0_ffn_in['Wg'], 'L0_ffn_Wq': _L0_ffn_in['Wq'], 'L0_ffn_Wk': _L0_ffn_in['Wk'], 'L0_ffn_Wv': _L0_ffn_in['Wv'], 'L0_ffn_Wo': _L0_ffn_in['Wo']}

def reference(x, adj, L0_gnn_weight, L0_gnn_wq, L0_gnn_wk, L0_ffn_Wg, L0_ffn_Wq, L0_ffn_Wk, L0_ffn_Wv, L0_ffn_Wo):
    import jax
    import jax.numpy as jnp

    def _L0_gnn_ref(feature, graph, weight, wq, wk):
        import jax, jax.numpy as jnp
        import numpy as np
        IN_DIM = 512
        OUT_DIM = 512
        BATCH = 128
        NUM_OBJS = 100
        output = jnp.einsum('bni,io->bno', feature, weight)
        q = jnp.einsum('bni,io->bno', feature, wq)
        k = jnp.einsum('bni,io->bno', feature, wk)
        alpha = jnp.einsum('bno,bmo->bnm', q, k)
        alpha = jnp.maximum(alpha, 0.0) * (graph != 0).astype(alpha.dtype)
        alpha = jax.nn.softmax(alpha, axis=1)
        return jnp.einsum('bnm,bmo->bno', alpha, output)

    def _L0_ffn_ref(token_inputs, Wg, Wq, Wk, Wv, Wo):
        import jax, jax.numpy as jnp
        import numpy as np
        CAPACITY_FACTOR = 0.5
        NUM_HEADS = 16
        B, N, D = token_inputs.shape
        C = int(N * CAPACITY_FACTOR)
        H = NUM_HEADS
        dh = D // H
        gate = jax.nn.sigmoid((token_inputs @ Wg)[..., 0])
        _, idx = jax.lax.top_k(gate, C)
        attn_in = jnp.take_along_axis(token_inputs, idx[..., None], axis=1)
        q = (attn_in @ Wq).reshape(B, C, H, dh)
        k = (attn_in @ Wk).reshape(B, C, H, dh)
        v = (attn_in @ Wv).reshape(B, C, H, dh)
        scores = jnp.einsum('bqhd,bkhd->bhqk', q, k) / jnp.sqrt(jnp.float32(dh))
        attn = jax.nn.softmax(scores, axis=-1)
        o = jnp.einsum('bhqk,bkhd->bqhd', attn, v).reshape(B, C, D) @ Wo
        gate_sel = jnp.take_along_axis(gate, idx, axis=1)
        out = jnp.zeros_like(token_inputs)
        out = out.at[jnp.arange(B)[:, None], idx].set(o * gate_sel[..., None])
        return out
    x = x + _L0_gnn_ref(_layernorm(x, axis=-1), adj, L0_gnn_weight, L0_gnn_wq, L0_gnn_wk)
    x = x + _L0_ffn_ref(_layernorm(x, axis=-1), L0_ffn_Wg, L0_ffn_Wq, L0_ffn_Wk, L0_ffn_Wv, L0_ffn_Wo)
    return x

_drawn_inputs = setup_inputs


def setup_inputs(seed=0):
    import zlib

    import numpy as np

    out = dict(_drawn_inputs(seed))
    spreads = {}
    factors = {}
    for name, (base, spread) in spreads.items():
        noise = np.random.default_rng([zlib.crc32(name.encode()), seed]).standard_normal(out[name].shape)
        drawn = base * np.exp(spread * noise) if base else spread * noise
        out[name] = jnp.asarray(drawn.astype(out[name].dtype))
    for name, factor in factors.items():
        out[name] = (out[name] * factor).astype(out[name].dtype)
    return out
```

```python
import math
from contextlib import ExitStack

import concourse.bass as bass
from concourse import mybir


def gnn_then_routed_attention(nc, x, adj_t, gnn_w, gnn_wq_t, gnn_wk_t, gate_w, wq, wk, wv, wo, out):
    fp32, fp16, i32 = mybir.dt.float32, mybir.dt.float16, mybir.dt.int32
    ALU, ACT, AX = mybir.AluOpType, mybir.ActivationFunctionType, mybir.AxisListType

    BATCHES, TOKENS, DIM = x.shape
    P = 128
    TC = TOKENS // P
    KC = DIM // P
    PICKED = TOKENS // 2
    HEADS = 16
    DH = DIM // HEADS
    GROUPS = P // DH
    EPS = 1e-5
    TINY = 2.0 ** -126
    FOLD = 2.0 ** -15
    assert PICKED == P and TC == 2 and KC == 4 and GROUPS == KC

    ctx = ExitStack()
    with ctx:
        def sb(name, shape, dt=fp32):
            return ctx.enter_context(nc.sbuf_tensor(name, shape, dt))

        def sem(name):
            return ctx.enter_context(nc.semaphore(name))

        def pair(name, shape):
            return [sb(f"{name}_hi", shape, fp16), sb(f"{name}_lo", shape, fp16)]

        NW = 7
        w_raw = sb("w_raw", [P, NW - 3, KC * DIM])
        w_split = [pair(f"w{i}", [P, KC, DIM]) for i in range(NW)]
        gnn_qk = pair("gnn_qk", [P, KC, DIM])
        w_max = sb("w_max", [P, NW])
        w_top = sb("w_top", [NW, 4])
        w_diag = sb("w_diag", [NW, 4, NW])
        w_bound = sb("w_bound", [P, NW])
        w_pow = sb("w_pow", [P, NW])
        w_rec = sb("w_rec", [P, NW])
        w_scale = sb("w_scale", [P, NW])
        unscale = sb("unscale", [P, 8])
        unscale_alpha = unscale[:, 1:2]
        unscale_w = unscale[:, 2:3]
        unscale_scores = unscale[:, 4:5]
        unscale_out = unscale[:, 6:7]
        gate_row = sb("gate_row", [P, DIM])
        ident = sb("ident", [P, P])
        ident16 = sb("ident16", [P, P], fp16)
        ones = sb("ones", [P, P])
        rank_row = sb("rank_row", [P, P])
        tie = sb("tie", [P, TC, TOKENS])
        half_neg = sb("half_neg", [P, TC])
        eps = sb("eps", [P, TC])

        x_in = [sb(f"x_in{i}", [P, TC, DIM]) for i in range(2)]
        adj_in = [sb(f"adj_in{i}", [P, TC, TOKENS], i32) for i in range(2)]
        x_mid = [sb(f"x_mid{i}", [P, TC, DIM]) for i in range(2)]
        stats = [sb(f"stats{i}", [P, TC, 6]) for i in range(2)]
        moments = [sb(f"moments{i}", [P, TC, 2]) for i in range(2)]
        var_eps = [sb(f"var_eps{i}", [P, TC]) for i in range(2)]
        rstd = [sb(f"rstd{i}", [P, TC]) for i in range(2)]
        xn = sb("xn", [P, TC, DIM])
        xn_t = pair("xn_t", [P, KC, TOKENS])
        xqk_t = pair("xqk_t", [P, KC, TOKENS])
        al_masked = sb("al_masked", [P, TC, TOKENS])
        al_relu = sb("al_relu", [P, TC, TOKENS])
        al_max = sb("al_max", [P, TC])
        al_bias = sb("al_bias", [P, TC])
        al_exp = sb("al_exp", [P, TC, TOKENS])
        al_sum = sb("al_sum", [P, TC])
        al_rec = sb("al_rec", [P, TC])
        alpha = pair("alpha", [P, TC, TOKENS])
        y = pair("y", [P, TC, DIM])
        xn2 = sb("xn2", [P, TC, DIM])
        xn2_s = pair("xn2_s", [P, TC, DIM])
        z_junk = sb("z_junk", [P, TC, DIM])
        z = sb("z", [P, TC])
        z_exp = sb("z_exp", [P, TC])
        z_den = sb("z_den", [P, TC])
        gate = sb("gate", [P, TC])
        gate_out = [sb(f"gate_out{i}", [P, TC]) for i in range(2)]
        cmp_junk = sb("cmp_junk", [P, TC, TOKENS], fp16)
        rank = sb("rank", [P, TC])
        pick = sb("pick", [P, TC, PICKED], fp16)
        pick_t = sb("pick_t", [P, TOKENS], fp16)
        sel_t = pair("sel_t", [P, KC, PICKED])
        q_t = pair("q_t", [P, KC, PICKED])
        k_t = pair("k_t", [P, KC, PICKED])
        v = pair("v", [P, HEADS, DH + 1])
        s_max = sb("s_max", [P, HEADS])
        s_bias = sb("s_bias", [P, HEADS])
        e = sb("e", [P, GROUPS, KC, PICKED])
        e_t = pair("e_t", [P, GROUPS, KC, PICKED])
        o_rec = sb("o_rec", [P, HEADS])
        o_norm = sb("o_norm", [P, HEADS, DH])
        o_t = pair("o_t", [P, KC, PICKED])
        proj = pair("proj", [P, DIM])

        banks = [ctx.enter_context(nc.psum_tensor(f"bank{i}", [P, DIM], fp32)) for i in range(8)]
        S, B = banks[:4], banks[4:]
        ps_xqk = [S[0], S[1]]
        ps_ot = S[2]
        ps_z = S[2]
        ps_pick_t = S[2][:, 0:TOKENS // 2].bitcast(fp16)
        ps_proj = S[3]
        ps_alpha = S[3]
        ps_scores = S
        ps_et = S
        ps_out = [B[0], B[1]]
        ps_sel = [B[2], B[3]]
        ps_q, ps_k, ps_v = B[2], B[3], B[0]
        ps_y = [B[1], B[2]]
        ps_xt = [B[3], B[0]]
        ps_msg = [B[1], B[2]]
        ps_o = [B[3], B[0]]

        consts_zeroed = sem("consts_zeroed")
        consts_ready = sem("consts_ready")
        w_max_ready = sem("w_max_ready")
        w_top_psum = sem("w_top_psum")
        w_top_ready = sem("w_top_ready")
        w_diag_ready = sem("w_diag_ready")
        w_bound_psum = sem("w_bound_psum")
        w_bound_ready = sem("w_bound_ready")
        w_pow_ready = sem("w_pow_ready")
        w_rec_ready = sem("w_rec_ready")
        w_scale_ready = sem("w_scale_ready")
        w_hi_ready = sem("w_hi_ready")
        w_lo_ready = sem("w_lo_ready")
        qk_psum = sem("qk_psum")
        qk_hi_ready = sem("qk_hi_ready")
        qk_lo_ready = sem("qk_lo_ready")
        unscale_ready = sem("unscale_ready")
        stats1_ready = sem("stats1_ready")
        moments1_ready = sem("moments1_ready")
        var1_ready = sem("var1_ready")
        rstd1_ready = sem("rstd1_ready")
        xn_ready = sem("xn_ready")
        stats2_ready = sem("stats2_ready")
        moments2_ready = sem("moments2_ready")
        var2_ready = sem("var2_ready")
        rstd2_ready = sem("rstd2_ready")
        xn2_ready = sem("xn2_ready")
        xn2_hi_ready = sem("xn2_hi_ready")
        xn2_lo_ready = sem("xn2_lo_ready")
        xt_psum = sem("xt_psum")
        xt_hi_ready = sem("xt_hi_ready")
        xt_lo_ready = sem("xt_lo_ready")
        xqk_psum = sem("xqk_psum")
        xqk_hi_ready = sem("xqk_hi_ready")
        xqk_lo_ready = sem("xqk_lo_ready")
        alpha_psum = sem("alpha_psum")
        al_masked_ready = sem("al_masked_ready")
        al_relu_ready = sem("al_relu_ready")
        al_bias_ready = sem("al_bias_ready")
        al_exp_ready = sem("al_exp_ready")
        al_rec_ready = sem("al_rec_ready")
        alpha_hi_ready = sem("alpha_hi_ready")
        alpha_lo_ready = sem("alpha_lo_ready")
        y_psum = sem("y_psum")
        y_hi_ready = sem("y_hi_ready")
        y_lo_ready = sem("y_lo_ready")
        msg_psum = sem("msg_psum")
        x_mid_ready = sem("x_mid_ready")
        z_ready = sem("z_ready")
        z_exp_ready = sem("z_exp_ready")
        z_den_ready = sem("z_den_ready")
        gate_ready = sem("gate_ready")
        gate_out_ready = sem("gate_out_ready")
        z_psum = sem("z_psum")
        rank_ready = sem("rank_ready")
        pick_ready = sem("pick_ready")
        sel_psum = sem("sel_psum")
        sel_hi_ready = sem("sel_hi_ready")
        sel_lo_ready = sem("sel_lo_ready")
        pick_psum = sem("pick_psum")
        pick_t_ready = sem("pick_t_ready")
        q_psum = sem("q_psum")
        q_hi_ready = sem("q_hi_ready")
        q_lo_ready = sem("q_lo_ready")
        k_psum = sem("k_psum")
        k_hi_ready = sem("k_hi_ready")
        k_lo_ready = sem("k_lo_ready")
        v_psum = sem("v_psum")
        v_hi_ready = sem("v_hi_ready")
        v_lo_ready = sem("v_lo_ready")
        scores_psum = sem("scores_psum")
        s_max_ready = sem("s_max_ready")
        s_bias_ready = sem("s_bias_ready")
        e_ready = sem("e_ready")
        et_psum = sem("et_psum")
        et_hi_ready = sem("et_hi_ready")
        et_lo_ready = sem("et_lo_ready")
        o_psum = sem("o_psum")
        o_rec_ready = sem("o_rec_ready")
        o_norm_ready = sem("o_norm_ready")
        ot_psum = sem("ot_psum")
        ot_hi_ready = sem("ot_hi_ready")
        ot_lo_ready = sem("ot_lo_ready")
        proj_psum = sem("proj_psum")
        proj_hi_ready = sem("proj_hi_ready")
        proj_lo_ready = sem("proj_lo_ready")
        out_psum = sem("out_psum")
        out_ready = sem("out_ready")
        gate_row_loaded = sem("gate_row_loaded")
        w_loaded = [sem(f"w{i}_loaded") for i in range(NW)]
        x_loaded = [sem(f"x_loaded{i}") for i in range(2)]
        adj_loaded = [sem(f"adj_loaded{i}") for i in range(2)]
        out_stored = [sem(f"out_stored{i}") for i in range(2)]

        WGROUPS = [(0, 2), (2, 3), (3, NW)]

        x_view = x.rearrange("b (c p) d -> b p c d", p=P)
        adj_view = adj_t.rearrange("b (c p) n -> b p c n", p=P)
        out_view = out.rearrange("b (c p) d -> b p c d", p=P)

        def periods(engine, period, between=None):
            period(0, 0, 0, gnn=True, attn=False, tail=False, nxt=True)
            if between:
                between()
            period(1, 0, 1, gnn=True, attn=True, tail=False, nxt=True)
            with engine.Fori(1, BATCHES // 2 - 1) as half:
                period(half * 2, half, 0, gnn=True, attn=True, tail=True, nxt=True)
                period(half * 2 + 1, half, 1, gnn=True, attn=True, tail=True, nxt=True)
            end = BATCHES // 2
            period(BATCHES - 2, end - 1, 0, gnn=True, attn=True, tail=True, nxt=True)
            period(BATCHES - 1, end - 1, 1, gnn=True, attn=True, tail=True, nxt=False)
            period(BATCHES, end, 0, gnn=False, attn=True, tail=True, nxt=False)
            period(BATCHES + 1, end, 1, gnn=False, attn=False, tail=True, nxt=False)

        def slot(half, par, back):
            return (par - back) % 2, half + (par - back) // 2

        block = ctx.enter_context(nc.Block())

        @block.sync
        def _(sp):
            def load_x(b, buf):
                sp.dma_start(x_in[buf][:, :, :], x_view[b]).then_inc(x_loaded[buf], 16)

            def load_adj(b, buf):
                sp.dma_start(adj_in[buf][:, :, :], adj_view[b]).then_inc(adj_loaded[buf], 16)

            def load_w(i, w):
                sp.dma_start(w_raw[:, i % 4, :].rearrange("p (k n) -> p k n", k=KC),
                             w.rearrange("(k p) n -> p k n", p=P)).then_inc(w_loaded[i], 16)

            load_x(0, 0)
            load_w(0, gnn_wq_t)
            load_w(1, gnn_wk_t)
            load_adj(0, 0)
            load_w(2, gnn_w)
            load_x(1, 1)
            load_adj(1, 1)
            sp.dma_start(gate_row[:, :], gate_w.partition_broadcast(P)).then_inc(gate_row_loaded, 16)
            for i, w in ((3, wq), (4, wk), (5, wv), (6, wo)):
                if i >= 4:
                    sp.wait_ge(w_lo_ready, i - 3)
                load_w(i, w)

            def period(t, half, par, gnn, attn, tail, nxt):
                if nxt and attn:
                    sp.wait_ge(x_mid_ready, (t - 1) * TC + TC)
                    load_x(t + 1, slot(half, par, -1)[0])
                if tail:
                    sp.wait_ge(out_ready, (t - 2) * TC + TC)
                    buf = slot(half, par, 2)[0]
                    sp.dma_start(out_view[t - 2], x_mid[buf][:, :, :]).then_inc(out_stored[buf], 16)
                if gnn and not (isinstance(t, int) and t + 2 >= BATCHES):
                    sp.wait_ge(al_masked_ready, t + 1)
                    load_adj(t + 2, slot(half, par, -2)[0])

            periods(sp, period)
            for buf in range(2):
                sp.wait_ge(out_stored[buf], 16 * (BATCHES // 2))

        @block.gpsimd
        def _(pool):
            pool.memset(half_neg[:, :], -0.5).then_inc(consts_zeroed, 1)
            pool.memset(eps[:, :], EPS).then_inc(consts_zeroed, 1)
            pool.memset(ident[:, :], 0.0).then_inc(consts_zeroed, 1)
            pool.memset(ident16[:, :], 0.0).then_inc(consts_zeroed, 1)
            pool.memset(tie[:, :, :], 0.0).then_inc(consts_zeroed, 1)
            pool.memset(v[1][:, :, :], 0.0).then_inc(consts_zeroed, 1)
            pool.memset(v[0][:, :, :], 1.0).then_inc(consts_zeroed, 1)
            pool.wait_ge(consts_zeroed, 7)
            for m in (ident, ident16):
                pool.affine_select(out=m[:, :], in_=m[:, :], compare_op=ALU.not_equal, fill=1.0, base=0,
                                   pattern=[[-1, P]], channel_multiplier=1).then_inc(consts_ready, 1)
            pool.memset(ones[:, :], 1.0).then_inc(consts_ready, 1)
            pool.iota(rank_row[:, :], pattern=[[1, P]], base=0, channel_multiplier=0,
                      allow_small_or_imprecise_dtypes=True).then_inc(consts_ready, 1)
            pool.affine_select(out=tie[:, :, :], in_=tie[:, :, :], compare_op=ALU.is_ge, fill=-TINY, base=0,
                               pattern=[[-P, TC], [1, TOKENS]], channel_multiplier=-1)\
                .then_inc(consts_ready, 1)

            def inverse_std(n, b, moments_ready, var_ready, rstd_ready):
                pool.wait_ge(moments_ready, b * TC + TC)
                pool.tensor_tensor(var_eps[n][:, :], moments[n][:, :, 1], eps[:, :], ALU.add)\
                    .then_inc(var_ready, 1)
                pool.wait_ge(var_ready, b + 1)
                pool.tensor_tensor(rstd[n][:, :], var_eps[n][:, :], half_neg[:, :], ALU.pow)\
                    .then_inc(rstd_ready, 1)

            inverse_std(0, 0, moments1_ready, var1_ready, rstd1_ready)

            def period(t, half, par, gnn, attn, tail, nxt):
                if attn:
                    inverse_std(1, t - 1, moments2_ready, var2_ready, rstd2_ready)
                    for c in range(TC):
                        pool.wait_ge(xn2_hi_ready, (t - 1) * TC + c + 1)
                        pool.tensor_tensor(xn2_s[1][:, c, :], xn2[:, c, :], xn2_s[0][:, c, :], ALU.subtract)\
                            .then_inc(xn2_lo_ready, 1)
                if nxt:
                    inverse_std(0, t + 1, moments1_ready, var1_ready, rstd1_ready)

            periods(pool, period)

        @block.scalar
        def _(act):
            def high(dst, src, psum_sem, count, done, scale=1.0):
                act.wait_ge(psum_sem, count)
                act.activation(dst, src, ACT.Copy, scale=scale).then_inc(done, 1)

            def weights_high(g):
                lo, up = WGROUPS[g]
                act.wait_ge(w_scale_ready, g + 1)
                for i in range(lo, up):
                    act.activation(w_split[i][0][:, :, :].rearrange("p k n -> p (k n)"), w_raw[:, i % 4, :],
                                   ACT.Copy, scale=w_scale[:, i:i + 1]).then_inc(w_hi_ready, 1)

            weights_high(0)
            for k in range(KC):
                high(gnn_qk[0][:, k, :], S[k][:, :], qk_psum, k + 1, qk_hi_ready, scale=FOLD)
            weights_high(1)
            for i in range(2):
                high(xn_t[0][:, 2 * i:2 * i + 2, :].rearrange("p k n -> p (k n)"), ps_xt[i][:, :],
                     xt_psum, i + 1, xt_hi_ready)

            def period(t, half, par, gnn, attn, tail, nxt):
                g, a, f = t, t - 1, t - 2
                if attn:
                    for c in range(TC):
                        act.wait_ge(xn2_ready, a * TC + c + 1)
                        act.activation(xn2_s[0][:, c, :], xn2[:, c, :], ACT.Copy).then_inc(xn2_hi_ready, 1)
                if tail:
                    high(o_t[0][:, :, :].rearrange("p k n -> p (k n)"), ps_ot[:, :], ot_psum, f + 1, ot_hi_ready)
                if gnn:
                    high(xqk_t[0][:, 0:2, :].rearrange("p k n -> p (k n)"), ps_xqk[0][:, :],
                         xqk_psum, g * 2 + 1, xqk_hi_ready)
                if attn:
                    act.wait_ge(z_ready, a * TC + TC)
                    act.activation(z_exp[:, :], z[:, :], ACT.Exp, scale=-1.0).then_inc(z_exp_ready, 1)
                if tail:
                    high(proj[0][:, :], ps_proj[:, :], proj_psum, f + 1, proj_hi_ready, scale=FOLD)
                if gnn:
                    high(xqk_t[0][:, 2:4, :].rearrange("p k n -> p (k n)"), ps_xqk[1][:, :],
                         xqk_psum, g * 2 + 2, xqk_hi_ready)
                if attn:
                    high(pick_t[:, :], ps_pick_t, pick_psum, a + 1, pick_t_ready)
                    high(sel_t[0][:, :, :].rearrange("p k n -> p (k n)"), ps_sel[0][:, :],
                         sel_psum, a * 2 + 1, sel_hi_ready)
                if gnn:
                    act.wait_ge(al_bias_ready, g + 1)
                    for c in range(TC):
                        act.activation(al_exp[:, c, :], al_relu[:, c, :], ACT.Exp, bias=al_bias[:, c:c + 1],
                                       scale=unscale_alpha, accum_out=al_sum[:, c:c + 1]).then_inc(al_exp_ready, 1)
                if attn:
                    high(q_t[0][:, :, :].rearrange("p k n -> p (k n)"), ps_q[:, :], q_psum, a + 1, q_hi_ready)
                    high(k_t[0][:, :, :].rearrange("p k n -> p (k n)"), ps_k[:, :], k_psum, a + 1, k_hi_ready)
                    high(v[0][:, :, 0:DH], ps_v[:, :].rearrange("p (h d) -> p h d", d=DH),
                         v_psum, a + 1, v_hi_ready)

                def exponentials(i):
                    act.wait_ge(s_bias_ready, a * GROUPS + i + 1)
                    for j in range(KC):
                        h = 4 * i + j
                        last = act.activation(e[:, i, j, :], ps_scores[i][:, j * P:j * P + P], ACT.Exp,
                                              bias=s_bias[:, h:h + 1], scale=unscale_scores)
                    last.then_inc(e_ready, 1)

                def y_high(c):
                    high(y[0][:, c, :], ps_y[c][:, :], y_psum, g * TC + c + 1, y_hi_ready)

                if attn:
                    exponentials(0)
                    exponentials(1)
                if gnn:
                    y_high(0)
                if attn:
                    exponentials(2)
                    exponentials(3)
                if gnn:
                    y_high(1)
                if nxt:
                    for i in range(2):
                        high(xn_t[0][:, 2 * i:2 * i + 2, :].rearrange("p k n -> p (k n)"), ps_xt[i][:, :],
                             xt_psum, (g + 1) * 2 + i + 1, xt_hi_ready)
                if attn:
                    for i in range(GROUPS):
                        high(e_t[0][:, i, :, :].rearrange("p k n -> p (k n)"), ps_et[i][:, :],
                             et_psum, a * GROUPS + i + 1, et_hi_ready)

            periods(act, period, between=lambda: weights_high(2))

        @block.vector
        def _(dve):
            def low(dst, src, hi, hi_sem, count, done, scale=None):
                dve.wait_ge(hi_sem, count)
                if scale is None:
                    ins = dve.tensor_tensor(dst, src, hi, ALU.subtract)
                else:
                    ins = dve.scalar_tensor_tensor(out=dst, in0=src, scalar=scale, in1=hi,
                                                   op0=ALU.mult, op1=ALU.subtract)
                ins.then_inc(done, 1)

            def weight_scales(g):
                lo, up = WGROUPS[g]
                n = up - lo
                for i in range(lo, up):
                    dve.wait_ge(w_loaded[i], 16)
                    last = dve.tensor_reduce(w_max[:, i:i + 1], w_raw[:, i % 4, :], AX.X, ALU.max,
                                             apply_absolute_value=True)
                last.then_inc(w_max_ready, 1)
                dve.wait_ge(w_top_psum, g + 1)
                dve.tensor_reduce(w_top[0:n, g:g + 1], S[2][0:n, 0:P], AX.X, ALU.max).then_inc(w_top_ready, 1)
                dve.wait_ge(w_top_ready, g + 1)
                dve.tensor_scalar(w_diag[0:n, g, 0:n], ident[0:n, 0:n], w_top[0:n, g:g + 1], None, ALU.mult)\
                    .then_inc(w_diag_ready, 1)
                dve.wait_ge(w_bound_psum, g + 1)
                dve.tensor_scalar(w_bound[:, lo:up], S[2][:, P:P + n], 1e-30, None, ALU.max)\
                    .then_inc(w_bound_ready, 1)
                dve.wait_ge(w_bound_ready, g + 1)
                dve.tensor_scalar(w_pow[:, lo:up].bitcast(i32), w_bound[:, lo:up].bitcast(i32), 0x7F800000, None,
                                  ALU.bitwise_and).then_inc(w_pow_ready, 1)
                dve.wait_ge(w_pow_ready, g + 1)
                dve.reciprocal(w_rec[:, lo:up], w_pow[:, lo:up]).then_inc(w_rec_ready, 1)
                dve.wait_ge(w_rec_ready, g + 1)
                dve.tensor_scalar(w_scale[:, lo:up], w_rec[:, lo:up], 32.0, None, ALU.mult)\
                    .then_inc(w_scale_ready, 1)
                dve.wait_ge(w_scale_ready, g + 1)
                for i in range(lo, up):
                    low(w_split[i][1][:, :, :].rearrange("p k n -> p (k n)"), w_raw[:, i % 4, :],
                        w_split[i][0][:, :, :].rearrange("p k n -> p (k n)"), w_hi_ready, i + 1, w_lo_ready,
                        scale=w_scale[:, i:i + 1])

            def moments_of(n, src, b, stats_ready, moments_ready):
                for c in range(TC):
                    dve.bn_stats(stats[n][:, c, :], src[:, c, :]).then_inc(stats_ready, 1)
                dve.drain()
                for c in range(TC):
                    dve.bn_aggr(moments[n][:, c, :], stats[n][:, c, :]).then_inc(moments_ready, 1)

            def normalise(n, dst, src, b, rstd_ready, done):
                dve.wait_ge(rstd_ready, b + 1)
                for c in range(TC):
                    dve.tensor_scalar(dst[:, c, :], src[:, c, :], moments[n][:, c, 0:1], rstd[n][:, c:c + 1],
                                      ALU.subtract, ALU.mult).then_inc(done, 1)

            def xt_low(b):
                for i in range(2):
                    low(xn_t[1][:, 2 * i:2 * i + 2, :].rearrange("p k n -> p (k n)"), ps_xt[i][:, :],
                        xn_t[0][:, 2 * i:2 * i + 2, :].rearrange("p k n -> p (k n)"),
                        xt_hi_ready, b * 2 + i + 1, xt_lo_ready)

            dve.wait_ge(x_loaded[0], 16)
            moments_of(0, x_in[0], 0, stats1_ready, moments1_ready)
            normalise(0, xn, x_in[0], 0, rstd1_ready, xn_ready)
            dve.wait_ge(consts_ready, 5)
            weight_scales(0)
            dve.scalar_tensor_tensor(out=unscale[:, 1:2], in0=w_pow[:, 0:1], scalar=1.0 / (1024.0 * FOLD),
                                     in1=w_pow[:, 1:2], op0=ALU.mult, op1=ALU.mult).then_inc(unscale_ready, 1)
            for k in range(KC):
                low(gnn_qk[1][:, k, :], S[k][:, :], gnn_qk[0][:, k, :], qk_hi_ready, k + 1, qk_lo_ready, scale=FOLD)
            weight_scales(1)
            dve.tensor_scalar(unscale[:, 2:3], w_pow[:, 2:3], 1.0 / 32.0, None, ALU.mult).then_inc(unscale_ready, 1)
            xt_low(0)

            def between():
                weight_scales(2)
                dve.scalar_tensor_tensor(out=unscale[:, 4:5], in0=w_pow[:, 3:4],
                                         scalar=1.0 / (1024.0 * math.sqrt(DH)), in1=w_pow[:, 4:5],
                                         op0=ALU.mult, op1=ALU.mult).then_inc(unscale_ready, 1)
                dve.scalar_tensor_tensor(out=unscale[:, 6:7], in0=w_pow[:, 5:6], scalar=1.0 / (1024.0 * FOLD),
                                         in1=w_pow[:, 6:7], op0=ALU.mult, op1=ALU.mult).then_inc(unscale_ready, 1)
                dve.wait_ge(unscale_ready, 4)

            def period(t, half, par, gnn, attn, tail, nxt):
                g, a, f = t, t - 1, t - 2
                buf_g, _ = slot(half, par, 0)
                buf_a, half_a = slot(half, par, 1)
                buf_f, _ = slot(half, par, 2)
                if attn:
                    if tail:
                        dve.wait_ge(out_stored[buf_a], half_a * 16)
                    for c in range(TC):
                        dve.wait_ge(msg_psum, a * TC + c + 1)
                        dve.scalar_tensor_tensor(out=x_mid[buf_a][:, c, :], in0=ps_msg[c][:, :], scalar=unscale_w,
                                                 in1=x_in[buf_a][:, c, :], op0=ALU.mult, op1=ALU.add)\
                            .then_inc(x_mid_ready, 1)
                    dve.wait_ge(x_mid_ready, a * TC + TC)
                    moments_of(1, x_mid[buf_a], a, stats2_ready, moments2_ready)
                if tail:
                    for i in range(2):
                        dve.wait_ge(o_psum, f * 2 + i + 1)
                        dve.reciprocal(o_rec[:, 8 * i:8 * i + 8],
                                       ps_o[i][:, 0:8 * (DH + 1)].rearrange("p (h d) -> p h d", d=DH + 1)[:, :, DH])\
                            .then_inc(o_rec_ready, 1)
                    for i in range(2):
                        dve.wait_ge(o_rec_ready, f * 2 + i + 1)
                        dve.tensor_tensor(
                            o_norm[:, 8 * i:8 * i + 8, :],
                            ps_o[i][:, 0:8 * (DH + 1)].rearrange("p (h d) -> p h d", d=DH + 1)[:, :, 0:DH],
                            o_rec[:, 8 * i:8 * i + 8].unsqueeze(2).to_broadcast([P, 8, DH]),
                            ALU.mult).then_inc(o_norm_ready, 1)
                if attn:
                    normalise(1, xn2, x_mid[buf_a], a, rstd2_ready, xn2_ready)
                    for c in range(TC):
                        dve.wait_ge(xn2_ready, a * TC + c + 1)
                        dve.scalar_tensor_tensor(out=z_junk[:, c, :], in0=xn2[:, c, :], scalar=1.0,
                                                 in1=gate_row[:, :], op0=ALU.mult, op1=ALU.mult,
                                                 accum_out=z[:, c:c + 1]).then_inc(z_ready, 1)
                if tail:
                    low(o_t[1][:, :, :].rearrange("p k n -> p (k n)"), ps_ot[:, :],
                        o_t[0][:, :, :].rearrange("p k n -> p (k n)"), ot_hi_ready, f + 1, ot_lo_ready)
                if gnn:
                    low(xqk_t[1][:, 0:2, :].rearrange("p k n -> p (k n)"), ps_xqk[0][:, :],
                        xqk_t[0][:, 0:2, :].rearrange("p k n -> p (k n)"), xqk_hi_ready, g * 2 + 1, xqk_lo_ready)
                if tail:
                    low(proj[1][:, :], ps_proj[:, :], proj[0][:, :], proj_hi_ready, f + 1, proj_lo_ready, scale=FOLD)
                if attn:
                    dve.wait_ge(z_psum, a + 1)
                    for c in range(TC):
                        dve.scalar_tensor_tensor(out=cmp_junk[:, c, :], in0=ps_z[:, 0:TOKENS], scalar=z[:, c:c + 1],
                                                 in1=tie[:, c, :], op0=ALU.subtract, op1=ALU.is_gt,
                                                 accum_out=rank[:, c:c + 1]).then_inc(rank_ready, 1)
                    for c in range(TC):
                        dve.wait_ge(rank_ready, a * TC + c + 1)
                        dve.tensor_scalar(pick[:, c, :], rank_row[:, :], rank[:, c:c + 1], None, ALU.is_equal)\
                            .then_inc(pick_ready, 1)
                if gnn:
                    low(xqk_t[1][:, 2:4, :].rearrange("p k n -> p (k n)"), ps_xqk[1][:, :],
                        xqk_t[0][:, 2:4, :].rearrange("p k n -> p (k n)"), xqk_hi_ready, g * 2 + 2, xqk_lo_ready)
                if tail:
                    for c in range(TC):
                        dve.wait_ge(out_psum, f * TC + c + 1)
                        dve.scalar_tensor_tensor(out=x_mid[buf_f][:, c, :], in0=ps_out[c][:, :],
                                                 scalar=gate_out[buf_f][:, c:c + 1], in1=x_mid[buf_f][:, c, :],
                                                 op0=ALU.mult, op1=ALU.add).then_inc(out_ready, 1)
                if attn:
                    dve.wait_ge(z_exp_ready, a + 1)
                    dve.tensor_scalar(z_den[:, :], z_exp[:, :], 1.0, None, ALU.add).then_inc(z_den_ready, 1)
                    dve.wait_ge(sel_psum, a * 2 + 2)
                    dve.tensor_copy(sel_t[1][:, :, :].rearrange("p k n -> p (k n)"), ps_sel[1][:, :])\
                        .then_inc(sel_lo_ready, 1)
                    dve.wait_ge(z_den_ready, a + 1)
                    dve.reciprocal(gate[:, :], z_den[:, :]).then_inc(gate_ready, 1)
                if gnn:
                    dve.wait_ge(alpha_psum, g + 1)
                    dve.wait_ge(adj_loaded[buf_g], half * 16 + 16)
                    dve.scalar_tensor_tensor(out=al_masked[:, :, :].rearrange("p c n -> p (c n)"),
                                             in0=adj_in[buf_g][:, :, :].rearrange("p c n -> p (c n)"), scalar=0.0,
                                             in1=ps_alpha[:, :], op0=ALU.not_equal, op1=ALU.mult)\
                        .then_inc(al_masked_ready, 1)
                    dve.wait_ge(al_masked_ready, g + 1)
                    for c in range(TC):
                        dve.tensor_scalar(al_relu[:, c, :], al_masked[:, c, :], 0.0, None, ALU.max, ALU.max,
                                          accum_out=al_max[:, c:c + 1]).then_inc(al_relu_ready, 1)
                    dve.wait_ge(al_relu_ready, g * TC + TC)
                    dve.tensor_scalar(al_bias[:, :], al_max[:, :], unscale_alpha, -1.0, ALU.mult, ALU.mult)\
                        .then_inc(al_bias_ready, 1)
                if attn:
                    dve.wait_ge(gate_ready, a + 1)
                    dve.tensor_scalar(gate_out[buf_a][:, :], gate[:, :], unscale_out, None, ALU.mult)\
                        .then_inc(gate_out_ready, 1)
                    low(q_t[1][:, :, :].rearrange("p k n -> p (k n)"), ps_q[:, :],
                        q_t[0][:, :, :].rearrange("p k n -> p (k n)"), q_hi_ready, a + 1, q_lo_ready)
                if gnn:
                    dve.wait_ge(al_exp_ready, g * TC + TC)
                    dve.reciprocal(al_rec[:, :], al_sum[:, :]).then_inc(al_rec_ready, 1)
                    dve.wait_ge(al_rec_ready, g + 1)
                    for c in range(TC):
                        dve.tensor_scalar(alpha[0][:, c, :], al_exp[:, c, :], al_rec[:, c:c + 1], None, ALU.mult)\
                            .then_inc(alpha_hi_ready, 1)
                    for c in range(TC):
                        low(alpha[1][:, c, :], al_exp[:, c, :], alpha[0][:, c, :], alpha_hi_ready,
                            g * TC + c + 1, alpha_lo_ready, scale=al_rec[:, c:c + 1])
                if attn:
                    low(k_t[1][:, :, :].rearrange("p k n -> p (k n)"), ps_k[:, :],
                        k_t[0][:, :, :].rearrange("p k n -> p (k n)"), k_hi_ready, a + 1, k_lo_ready)
                    low(v[1][:, :, 0:DH], ps_v[:, :].rearrange("p (h d) -> p h d", d=DH), v[0][:, :, 0:DH],
                        v_hi_ready, a + 1, v_lo_ready)
                if nxt:
                    buf_n, half_n = slot(half, par, -1)
                    dve.wait_ge(x_loaded[buf_n], half_n * 16 + 16)
                    moments_of(0, x_in[buf_n], g + 1, stats1_ready, moments1_ready)
                    normalise(0, xn, x_in[buf_n], g + 1, rstd1_ready, xn_ready)
                if attn:
                    dve.wait_ge(scores_psum, a + 1)
                    for i in range(GROUPS):
                        dve.tensor_reduce(s_max[:, 4 * i:4 * i + 4],
                                          ps_scores[i][:, :].rearrange("p (j n) -> p j n", n=P), AX.X, ALU.max)\
                            .then_inc(s_max_ready, 1)
                        dve.wait_ge(s_max_ready, a * GROUPS + i + 1)
                        dve.tensor_scalar(s_bias[:, 4 * i:4 * i + 4], s_max[:, 4 * i:4 * i + 4], unscale_scores, -1.0,
                                          ALU.mult, ALU.mult).then_inc(s_bias_ready, 1)
                if gnn:
                    for c in range(TC):
                        low(y[1][:, c, :], ps_y[c][:, :], y[0][:, c, :], y_hi_ready, g * TC + c + 1, y_lo_ready)
                if nxt:
                    xt_low(g + 1)
                if attn:
                    for i in range(GROUPS):
                        low(e_t[1][:, i, :, :].rearrange("p k n -> p (k n)"), ps_et[i][:, :],
                            e_t[0][:, i, :, :].rearrange("p k n -> p (k n)"), et_hi_ready,
                            a * GROUPS + i + 1, et_lo_ready)

            dve.wait_ge(unscale_ready, 2)
            dve.wait_ge(gate_row_loaded, 16)
            periods(dve, period, between=between)

        @block.tensor
        def _(pe):
            PASSES = ((0, 0), (0, 1), (1, 0))

            def product(dst, steps, lhs, rhs):
                for n, (l, r) in enumerate(PASSES):
                    for k in range(steps):
                        last = pe.matmul(dst, lhs(l, k), rhs(r, k), start=(n == 0 and k == 0),
                                         stop=(n == 2 and k == steps - 1))
                return last

            def weight_bounds(g):
                lo, up = WGROUPS[g]
                n = up - lo
                pe.wait_ge(w_max_ready, g + 1)
                pe.transpose(S[2][0:n, 0:P], w_max[:, lo:up], ident[:, :]).then_inc(w_top_psum, 1)
                pe.wait_ge(w_diag_ready, g + 1)
                pe.matmul(S[2][:, P:P + n], ones[0:n, :], w_diag[0:n, g, 0:n], start=True, stop=True)\
                    .then_inc(w_bound_psum, 1)

            def transpose_x(b):
                pe.wait_ge(xn_ready, b * TC + TC)
                for i in range(2):
                    for k in (2 * i, 2 * i + 1):
                        for c in range(TC):
                            at = (k % 2) * TOKENS + c * P
                            last = pe.transpose(ps_xt[i][:, at:at + P], xn[:, c, k * P:k * P + P], ident[:, :])
                    last.then_inc(xt_psum, 1)

            pe.wait_ge(consts_ready, 5)
            transpose_x(0)
            weight_bounds(0)
            pe.wait_ge(w_lo_ready, 2)
            pe.wait_ge(w_bound_ready, 1)
            for k in range(KC):
                product(S[k][:, :], KC, lambda p, o: w_split[0][p][:, o, k * P:k * P + P],
                        lambda p, o: w_split[1][p][:, o, :]).then_inc(qk_psum, 1)
            pe.wait_ge(qk_lo_ready, KC)
            weight_bounds(1)

            def period(t, half, par, gnn, attn, tail, nxt):
                g, a, f = t, t - 1, t - 2
                if gnn:
                    pe.wait_ge(xt_lo_ready, g * 2 + 2)
                    product(ps_xqk[0][:, 0:TOKENS], KC, lambda p, k: gnn_qk[p][:, k, 0:P], lambda p, k: xn_t[p][:, k, :])
                if tail:
                    pe.wait_ge(o_norm_ready, f * 2 + 2)
                    for k in range(KC):
                        last = pe.transpose(ps_ot[:, k * P:k * P + P],
                                            o_norm[:, :, :].rearrange("p h d -> p (h d)")[:, k * P:k * P + P],
                                            ident[:, :])
                    last.then_inc(ot_psum, 1)
                if gnn:
                    product(ps_xqk[0][:, TOKENS:2 * TOKENS], KC, lambda p, k: gnn_qk[p][:, k, P:2 * P],
                            lambda p, k: xn_t[p][:, k, :]).then_inc(xqk_psum, 1)
                if tail:
                    pe.wait_ge(ot_lo_ready, f + 1)
                    product(ps_proj[:, :], KC, lambda p, k: o_t[p][:, k, :], lambda p, k: w_split[6][p][:, k, :])\
                        .then_inc(proj_psum, 1)
                if gnn:
                    product(ps_xqk[1][:, 0:TOKENS], KC, lambda p, k: gnn_qk[p][:, k, 2 * P:3 * P],
                            lambda p, k: xn_t[p][:, k, :])
                if attn:
                    pe.wait_ge(z_ready, a * TC + TC)
                    for c in range(TC):
                        last = pe.transpose(ps_z[:, c * P:c * P + P], z[:, c:c + 1].to_broadcast([P, P]), ident[:, :])
                    last.then_inc(z_psum, 1)
                if tail:
                    pe.wait_ge(proj_lo_ready, f + 1)
                    for c in range(TC):
                        for p in range(2):
                            last = pe.matmul(ps_out[c][:, :], pick_t[:, c * P:c * P + P], proj[p][:, :],
                                             start=(p == 0), stop=(p == 1))
                        last.then_inc(out_psum, 1)
                if gnn:
                    product(ps_xqk[1][:, TOKENS:2 * TOKENS], KC, lambda p, k: gnn_qk[p][:, k, 3 * P:4 * P],
                            lambda p, k: xn_t[p][:, k, :]).then_inc(xqk_psum, 1)
                if attn:
                    pe.wait_ge(pick_ready, a * TC + TC)
                    for c in range(TC):
                        last = pe.transpose(ps_pick_t[:, c * P:c * P + P], pick[:, c, :], ident16[:, :])
                    last.then_inc(pick_psum, 1)
                    pe.wait_ge(xn2_lo_ready, a * TC + TC)
                    for p in range(2):
                        for k in range(KC):
                            for c in range(TC):
                                last = pe.matmul(ps_sel[p][:, k * P:k * P + P], xn2_s[p][:, c, k * P:k * P + P],
                                                 pick[:, c, :], start=(c == 0), stop=(c == TC - 1))
                        last.then_inc(sel_psum, 1)
                if gnn:
                    pe.wait_ge(xqk_lo_ready, g * 2 + 2)
                    for m in range(TC):
                        last = product(ps_alpha[:, m * TOKENS:(m + 1) * TOKENS], KC,
                                       lambda p, k: xn_t[p][:, k, m * P:m * P + P], lambda p, k: xqk_t[p][:, k, :])
                    last.then_inc(alpha_psum, 1)
                if attn:
                    pe.wait_ge(sel_hi_ready, a + 1)
                    pe.wait_ge(sel_lo_ready, a + 1)
                    for w, ps, done in ((3, ps_q, q_psum), (4, ps_k, k_psum)):
                        for j in range(KC):
                            last = product(ps[:, j * P:j * P + P], KC, lambda p, k: w_split[w][p][:, k, j * P:j * P + P],
                                           lambda p, k: sel_t[p][:, k, :])
                        last.then_inc(done, 1)
                    if tail:
                        pe.wait_ge(out_ready, f * TC + 1)
                    product(ps_v[:, :], KC, lambda p, k: sel_t[p][:, k, :], lambda p, k: w_split[5][p][:, k, :])\
                        .then_inc(v_psum, 1)
                    pe.wait_ge(q_lo_ready, a + 1)
                    pe.wait_ge(k_lo_ready, a + 1)
                    pe.wait_ge(pick_t_ready, a + 1)
                    if gnn:
                        pe.wait_ge(al_masked_ready, g + 1)
                    for j in range(KC):
                        for n, (l, r) in enumerate(PASSES):
                            for i in range(GROUPS):
                                rows = slice(i * DH, i * DH + DH)
                                last = pe.matmul(ps_scores[i][:, j * P:j * P + P], q_t[l][rows, j, :], k_t[r][rows, j, :],
                                                 start=(n == 0), stop=(n == 2))
                    last.then_inc(scores_psum, 1)
                if gnn:
                    if tail:
                        pe.wait_ge(out_ready, f * TC + TC)
                    for m in range(TC):
                        product(ps_y[m][:, :], KC, lambda p, k: xn_t[p][:, k, m * P:m * P + P],
                                lambda p, k: w_split[2][p][:, k, :]).then_inc(y_psum, 1)
                if nxt:
                    if attn:
                        pe.wait_ge(v_lo_ready, a + 1)
                    transpose_x(g + 1)
                if attn:
                    for i in range(GROUPS):
                        pe.wait_ge(e_ready, a * GROUPS + i + 1)
                        for j in range(KC):
                            last = pe.transpose(ps_et[i][:, j * P:j * P + P], e[:, i, j, :], ident[:, :])
                        last.then_inc(et_psum, 1)
                if gnn:
                    pe.wait_ge(y_lo_ready, g * TC + TC)
                    pe.wait_ge(alpha_lo_ready, g * TC + TC)
                    for c in range(TC):
                        product(ps_msg[c][:, :], TC, lambda p, m: alpha[p][:, m, c * P:c * P + P],
                                lambda p, m: y[p][:, m, :]).then_inc(msg_psum, 1)
                if attn:
                    pe.wait_ge(et_lo_ready, a * GROUPS + GROUPS)
                    pe.wait_ge(v_lo_ready, a + 1)
                    if nxt:
                        pe.wait_ge(xt_lo_ready, (g + 1) * 2 + 2)
                    for i in range(2):
                        for h in range(8 * i, 8 * i + 8):
                            at = (h - 8 * i) * (DH + 1)
                            last = product(ps_o[i][:, at:at + DH + 1], 1,
                                           lambda p, k: e_t[p][:, h % GROUPS, h // GROUPS, :],
                                           lambda p, k: v[p][:, h, :])
                        last.then_inc(o_psum, 1)

            def before_period_0():
                pe.wait_ge(w_lo_ready, 3)

            before_period_0()

            def between():
                weight_bounds(2)
                pe.wait_ge(w_lo_ready, NW)

            periods(pe, period, between=between)


_NAMES = ["x", "adj_t", "gnn_w", "gnn_wq_t", "gnn_wk_t", "gate_w", "wq", "wk", "wv", "wo"]


def kernel(x, adj, L0_gnn_weight, L0_gnn_wq, L0_gnn_wk, L0_ffn_Wg, L0_ffn_Wq, L0_ffn_Wk, L0_ffn_Wv, L0_ffn_Wo):
    import numpy as _np
    import concourse.bacc as _bacc
    from concourse import mybir as _mybir
    from concourse.bass_utils import run_bass_kernel_spmd as _run

    given = [
        _np.asarray(x), _np.asarray(adj).transpose(0, 2, 1), _np.asarray(L0_gnn_weight),
        _np.asarray(L0_gnn_wq).T, _np.asarray(L0_gnn_wk).T, _np.asarray(L0_ffn_Wg).reshape(-1),
        _np.asarray(L0_ffn_Wq), _np.asarray(L0_ffn_Wk), _np.asarray(L0_ffn_Wv), _np.asarray(L0_ffn_Wo),
    ]
    nc = _bacc.Bacc("TRN2", target_bir_lowering=False, num_devices=1)
    arrays, args = {}, []
    for name, a in zip(_NAMES, given):
        a = _np.ascontiguousarray(a)
        arrays[f"in_{name}"] = a
        args.append(nc.dram_tensor(f"in_{name}", a.shape, _mybir.dt.from_np(a.dtype), kind="ExternalInput").ap())
    args.append(nc.dram_tensor("out_0", given[0].shape, _mybir.dt.float32, kind="ExternalOutput").ap())
    gnn_then_routed_attention(nc, *args)
    result = _run(nc, [arrays], core_ids=[0])
    return result.results[0]["out_0"]
```

```python
import math
from contextlib import ExitStack

import concourse.bass as bass
from concourse import mybir


def gnn_then_routed_attention(nc, x, adj_t, gnn_w, gnn_wq_t, gnn_wk_t, gate_w, wq, wk, wv, wo, out):
    fp32, fp16, i32 = mybir.dt.float32, mybir.dt.float16, mybir.dt.int32
    ALU, ACT, AX = mybir.AluOpType, mybir.ActivationFunctionType, mybir.AxisListType

    BATCHES, TOKENS, DIM = x.shape
    P = 128
    TC = TOKENS // P
    KC = DIM // P
    PICKED = TOKENS // 2
    HEADS = 16
    DH = DIM // HEADS
    GROUPS = P // DH
    EPS = 1e-5
    TINY = 2.0 ** -126
    FOLD = 2.0 ** -15
    assert PICKED == P and TC == 2 and KC == 4 and GROUPS == KC

    ctx = ExitStack()
    with ctx:
        def sb(name, shape, dt=fp32):
            return ctx.enter_context(nc.sbuf_tensor(name, shape, dt))

        def sem(name):
            return ctx.enter_context(nc.semaphore(name))

        def pair(name, shape):
            return [sb(f"{name}_hi", shape, fp16), sb(f"{name}_lo", shape, fp16)]

        NW = 7
        w_raw = sb("w_raw", [P, NW - 3, KC * DIM])
        w_split = [pair(f"w{i}", [P, KC, DIM]) for i in range(NW)]
        gnn_qk = pair("gnn_qk", [P, KC, DIM])
        w_max = sb("w_max", [P, NW])
        w_top = sb("w_top", [2, 4])
        w_diag = sb("w_diag", [2, 4, 2])
        w_bound = sb("w_bound", [P, NW])
        w_pow = sb("w_pow", [P, NW])
        w_rec = sb("w_rec", [P, NW])
        w_scale = sb("w_scale", [P, NW])
        unscale = sb("unscale", [P, 8])
        unscale_alpha = unscale[:, 1:2]
        unscale_w = unscale[:, 2:3]
        unscale_scores = unscale[:, 4:5]
        unscale_out = unscale[:, 6:7]
        gate_row = sb("gate_row", [P, DIM])
        ident = sb("ident", [P, P])
        ident16 = sb("ident16", [P, P], fp16)
        ones = sb("ones", [P, P])
        rank_row = sb("rank_row", [P, P])
        tie = sb("tie", [P, TC, TOKENS])
        half_neg = sb("half_neg", [P, TC])
        eps = sb("eps", [P, TC])

        x_in = [sb(f"x_in{i}", [P, TC, DIM]) for i in range(2)]
        adj_in = [sb(f"adj_in{i}", [P, TC, TOKENS], i32) for i in range(2)]
        x_mid = [sb(f"x_mid{i}", [P, TC, DIM]) for i in range(2)]
        stats = [sb(f"stats{i}", [P, TC, 6]) for i in range(2)]
        moments = [sb(f"moments{i}", [P, TC, 2]) for i in range(2)]
        var_eps = [sb(f"var_eps{i}", [P, TC]) for i in range(2)]
        rstd = [sb(f"rstd{i}", [P, TC]) for i in range(2)]
        xn = sb("xn", [P, TC, DIM])
        xn_t = [pair(f"xn_t{i}", [P, KC, TOKENS]) for i in range(2)]
        xqk_t = pair("xqk_t", [P, KC, TOKENS])
        al_masked = sb("al_masked", [P, TC, TOKENS])
        al_relu = sb("al_relu", [P, TC, TOKENS])
        al_max = sb("al_max", [P, TC])
        al_bias = sb("al_bias", [P, TC])
        al_exp = sb("al_exp", [P, TC, TOKENS])
        al_sum = sb("al_sum", [P, TC])
        al_rec = sb("al_rec", [P, TC])
        alpha = pair("alpha", [P, TC, TOKENS])
        y = pair("y", [P, TC, DIM])
        xn2 = sb("xn2", [P, TC, DIM])
        xn2_s = pair("xn2_s", [P, TC, DIM])
        z_junk = sb("z_junk", [P, TC, DIM])
        z = sb("z", [P, TC])
        z_exp = sb("z_exp", [P, TC])
        z_den = sb("z_den", [P, TC])
        gate = sb("gate", [P, TC])
        gate_out = [sb(f"gate_out{i}", [P, TC]) for i in range(2)]
        cmp_junk = sb("cmp_junk", [P, TC, TOKENS], fp16)
        rank = sb("rank", [P, TC])
        pick = sb("pick", [P, TC, PICKED], fp16)
        pick_t = sb("pick_t", [P, TOKENS], fp16)
        sel_t = pair("sel_t", [P, KC, PICKED])
        q_t = pair("q_t", [P, KC, PICKED])
        k_t = pair("k_t", [P, KC, PICKED])
        v = pair("v", [P, HEADS, DH + 1])
        s_max = sb("s_max", [P, HEADS])
        s_bias = sb("s_bias", [P, HEADS])
        e = sb("e", [P, GROUPS, KC, PICKED])
        e_t = pair("e_t", [P, GROUPS, KC, PICKED])
        o_rec = sb("o_rec", [P, HEADS])
        o_norm = sb("o_norm", [P, HEADS, DH])
        o_t = pair("o_t", [P, KC, PICKED])
        proj = pair("proj", [P, DIM])

        banks = [ctx.enter_context(nc.psum_tensor(f"bank{i}", [P, DIM], fp32)) for i in range(8)]
        S, B = banks[:4], banks[4:]
        ps_xqk = [S[0], S[1]]
        ps_ot = S[2]
        ps_z = S[2]
        ps_pick_t = S[2][:, 0:TOKENS // 2].bitcast(fp16)
        ps_proj = S[3]
        ps_alpha = S[3]
        ps_scores = S
        ps_et = S
        ps_out = [B[0], B[1]]
        ps_sel = [B[2], B[3]]
        ps_q, ps_k, ps_v = B[2], B[3], B[0]
        ps_y = [B[1], B[2]]
        ps_xt = [B[0], B[1]]
        ps_msg = [B[1], B[2]]
        ps_o = [B[3], B[0]]
        ps_bound = [B[2], B[2], S[2], S[2]]

        consts_zeroed = sem("consts_zeroed")
        consts_ready = sem("consts_ready")
        w_max_ready = sem("w_max_ready")
        w_top_psum = sem("w_top_psum")
        w_top_ready = sem("w_top_ready")
        w_diag_ready = sem("w_diag_ready")
        w_bound_psum = sem("w_bound_psum")
        w_bound_ready = sem("w_bound_ready")
        w_pow_ready = sem("w_pow_ready")
        w_rec_ready = sem("w_rec_ready")
        w_scale_ready = sem("w_scale_ready")
        w_hi_ready = sem("w_hi_ready")
        w_lo_ready = sem("w_lo_ready")
        w1_hi_ready = sem("w1_hi_ready")
        w_scaled_ready = sem("w_scaled_ready")
        w_low_by_pool = sem("w_low_by_pool")
        qk_psum = sem("qk_psum")
        qk_hi_ready = sem("qk_hi_ready")
        qk_lo_ready = sem("qk_lo_ready")
        unscale_ready = sem("unscale_ready")
        stats1_ready = sem("stats1_ready")
        moments1_ready = sem("moments1_ready")
        var1_ready = sem("var1_ready")
        rstd1_ready = sem("rstd1_ready")
        xn_ready = sem("xn_ready")
        stats2_ready = sem("stats2_ready")
        moments2_ready = sem("moments2_ready")
        var2_ready = sem("var2_ready")
        rstd2_ready = sem("rstd2_ready")
        xn2_ready = sem("xn2_ready")
        xn2_hi_ready = sem("xn2_hi_ready")
        xn2_lo_ready = sem("xn2_lo_ready")
        xt_psum = sem("xt_psum")
        xt_hi_ready = sem("xt_hi_ready")
        xt_lo_ready = sem("xt_lo_ready")
        xqk_psum = sem("xqk_psum")
        xqk_hi_ready = sem("xqk_hi_ready")
        xqk_lo_ready = sem("xqk_lo_ready")
        alpha_psum = sem("alpha_psum")
        al_masked_ready = sem("al_masked_ready")
        al_relu_ready = sem("al_relu_ready")
        al_bias_ready = sem("al_bias_ready")
        al_exp_ready = sem("al_exp_ready")
        al_rec_ready = sem("al_rec_ready")
        alpha_hi_ready = sem("alpha_hi_ready")
        alpha_lo_ready = sem("alpha_lo_ready")
        y_psum = sem("y_psum")
        y_hi_ready = sem("y_hi_ready")
        y_lo_ready = sem("y_lo_ready")
        msg_psum = sem("msg_psum")
        x_mid_ready = sem("x_mid_ready")
        z_ready = sem("z_ready")
        z_exp_ready = sem("z_exp_ready")
        z_den_ready = sem("z_den_ready")
        gate_ready = sem("gate_ready")
        gate_out_ready = sem("gate_out_ready")
        z_psum = sem("z_psum")
        rank_ready = sem("rank_ready")
        pick_ready = sem("pick_ready")
        sel_psum = sem("sel_psum")
        sel_hi_ready = sem("sel_hi_ready")
        sel_lo_ready = sem("sel_lo_ready")
        pick_psum = sem("pick_psum")
        pick_t_ready = sem("pick_t_ready")
        q_psum = sem("q_psum")
        q_hi_ready = sem("q_hi_ready")
        q_lo_ready = sem("q_lo_ready")
        k_psum = sem("k_psum")
        k_hi_ready = sem("k_hi_ready")
        k_lo_ready = sem("k_lo_ready")
        v_psum = sem("v_psum")
        v_hi_ready = sem("v_hi_ready")
        v_lo_ready = sem("v_lo_ready")
        scores_psum = sem("scores_psum")
        s_max_ready = sem("s_max_ready")
        s_bias_ready = sem("s_bias_ready")
        e_ready = sem("e_ready")
        et_psum = sem("et_psum")
        et_hi_ready = sem("et_hi_ready")
        et_lo_ready = sem("et_lo_ready")
        o_psum = sem("o_psum")
        o_rec_ready = sem("o_rec_ready")
        o_norm_ready = sem("o_norm_ready")
        ot_psum = sem("ot_psum")
        ot_hi_ready = sem("ot_hi_ready")
        ot_lo_ready = sem("ot_lo_ready")
        proj_psum = sem("proj_psum")
        proj_hi_ready = sem("proj_hi_ready")
        proj_lo_ready = sem("proj_lo_ready")
        out_psum = sem("out_psum")
        out_ready = sem("out_ready")
        gate_row_loaded = sem("gate_row_loaded")
        w_loaded = [sem(f"w{i}_loaded") for i in range(NW)]
        x_loaded = [sem(f"x_loaded{i}") for i in range(2)]
        adj_loaded = [sem(f"adj_loaded{i}") for i in range(2)]
        out_stored = [sem(f"out_stored{i}") for i in range(2)]

        WGROUPS = [(0, 2), (2, 3), (3, 5), (5, NW)]

        x_view = x.rearrange("b (c p) d -> b p c d", p=P)
        adj_view = adj_t.rearrange("b (c p) n -> b p c n", p=P)
        out_view = out.rearrange("b (c p) d -> b p c d", p=P)

        def periods(engine, period):
            period(0, 0, 0, gnn=True, attn=False, tail=False, nxt=True)
            period(1, 0, 1, gnn=True, attn=True, tail=False, nxt=True)
            with engine.Fori(1, BATCHES // 2 - 1) as half:
                period(half * 2, half, 0, gnn=True, attn=True, tail=True, nxt=True)
                period(half * 2 + 1, half, 1, gnn=True, attn=True, tail=True, nxt=True)
            end = BATCHES // 2
            period(BATCHES - 2, end - 1, 0, gnn=True, attn=True, tail=True, nxt=True)
            period(BATCHES - 1, end - 1, 1, gnn=True, attn=True, tail=True, nxt=False)
            period(BATCHES, end, 0, gnn=False, attn=True, tail=True, nxt=False)
            period(BATCHES + 1, end, 1, gnn=False, attn=False, tail=True, nxt=False)

        def first(t):
            return isinstance(t, int) and t == 0

        def second(t):
            return isinstance(t, int) and t == 1

        def slot(half, par, back):
            return (par - back) % 2, half + (par - back) // 2

        block = ctx.enter_context(nc.Block())

        @block.sync
        def _(sp):
            def load_x(b, buf):
                sp.dma_start(x_in[buf][:, :, :], x_view[b]).then_inc(x_loaded[buf], 16)

            def load_adj(b, buf):
                sp.dma_start(adj_in[buf][:, :, :], adj_view[b]).then_inc(adj_loaded[buf], 16)

            def load_w(i, w):
                sp.dma_start(w_raw[:, i % 4, :].rearrange("p (k n) -> p k n", k=KC),
                             w.rearrange("(k p) n -> p k n", p=P)).then_inc(w_loaded[i], 16)

            load_w(0, gnn_wq_t)
            load_w(1, gnn_wk_t)
            load_x(0, 0)
            load_adj(0, 0)
            load_w(2, gnn_w)
            load_x(1, 1)
            load_adj(1, 1)
            sp.dma_start(gate_row[:, :], gate_w.partition_broadcast(P)).then_inc(gate_row_loaded, 16)
            for i, w in ((3, wq), (4, wk), (5, wv), (6, wo)):
                if i >= 4:
                    sp.wait_ge(w_lo_ready, i - 3)
                load_w(i, w)

            def period(t, half, par, gnn, attn, tail, nxt):
                if nxt and attn:
                    sp.wait_ge(x_mid_ready, (t - 1) * TC + TC)
                    load_x(t + 1, slot(half, par, -1)[0])
                if tail:
                    sp.wait_ge(out_ready, (t - 2) * TC + TC)
                    buf = slot(half, par, 2)[0]
                    sp.dma_start(out_view[t - 2], x_mid[buf][:, :, :]).then_inc(out_stored[buf], 16)
                if gnn and not (isinstance(t, int) and t + 2 >= BATCHES):
                    sp.wait_ge(al_masked_ready, t + 1)
                    load_adj(t + 2, slot(half, par, -2)[0])

            periods(sp, period)
            for buf in range(2):
                sp.wait_ge(out_stored[buf], 16 * (BATCHES // 2))

        @block.gpsimd
        def _(pool):
            pool.memset(half_neg[:, :], -0.5).then_inc(consts_zeroed, 1)
            pool.memset(eps[:, :], EPS).then_inc(consts_zeroed, 1)
            pool.memset(ident[:, :], 0.0).then_inc(consts_zeroed, 1)
            pool.memset(ident16[:, :], 0.0).then_inc(consts_zeroed, 1)
            pool.memset(tie[:, :, :], 0.0).then_inc(consts_zeroed, 1)
            pool.memset(v[1][:, :, :], 0.0).then_inc(consts_zeroed, 1)
            pool.memset(v[0][:, :, :], 1.0).then_inc(consts_zeroed, 1)
            pool.wait_ge(consts_zeroed, 7)
            for m in (ident, ident16):
                pool.affine_select(out=m[:, :], in_=m[:, :], compare_op=ALU.not_equal, fill=1.0, base=0,
                                   pattern=[[-1, P]], channel_multiplier=1).then_inc(consts_ready, 1)
            pool.memset(ones[:, :], 1.0).then_inc(consts_ready, 1)
            pool.iota(rank_row[:, :], pattern=[[1, P]], base=0, channel_multiplier=0,
                      allow_small_or_imprecise_dtypes=True).then_inc(consts_ready, 1)
            pool.affine_select(out=tie[:, :, :], in_=tie[:, :, :], compare_op=ALU.is_ge, fill=-TINY, base=0,
                               pattern=[[-P, TC], [1, TOKENS]], channel_multiplier=-1)\
                .then_inc(consts_ready, 1)

            def inverse_std(n, b, moments_ready, var_ready, rstd_ready):
                pool.wait_ge(moments_ready, b * TC + TC)
                pool.tensor_tensor(var_eps[n][:, :], moments[n][:, :, 1], eps[:, :], ALU.add)\
                    .then_inc(var_ready, 1)
                pool.wait_ge(var_ready, b + 1)
                pool.tensor_tensor(rstd[n][:, :], var_eps[n][:, :], half_neg[:, :], ALU.pow)\
                    .then_inc(rstd_ready, 1)

            inverse_std(0, 0, moments1_ready, var1_ready, rstd1_ready)

            def weight_low(i):
                pool.wait_ge(w_hi_ready, i)
                pool.tensor_tensor(w_split[i][1][:, :, :].rearrange("p k n -> p (k n)"), w_raw[:, i % 4, :],
                                   w_split[i][0][:, :, :].rearrange("p k n -> p (k n)"), ALU.subtract)\
                    .then_inc(w_low_by_pool, 1)

            def period(t, half, par, gnn, attn, tail, nxt):
                if attn:
                    inverse_std(1, t - 1, moments2_ready, var2_ready, rstd2_ready)
                    for c in range(TC):
                        pool.wait_ge(xn2_hi_ready, (t - 1) * TC + c + 1)
                        pool.tensor_tensor(xn2_s[1][:, c, :], xn2[:, c, :], xn2_s[0][:, c, :], ALU.subtract)\
                            .then_inc(xn2_lo_ready, 1)
                if nxt:
                    inverse_std(0, t + 1, moments1_ready, var1_ready, rstd1_ready)
                if first(t):
                    weight_low(3)
                    weight_low(4)
                if second(t):
                    weight_low(5)
                    weight_low(6)

            periods(pool, period)

        @block.scalar
        def _(act):
            def high(dst, src, psum_sem, count, done, scale=1.0):
                act.wait_ge(psum_sem, count)
                act.activation(dst, src, ACT.Copy, scale=scale).then_inc(done, 1)

            def weight_high(i, g):
                act.wait_ge(w_scale_ready, g + 1)
                act.activation(w_split[i][0][:, :, :].rearrange("p k n -> p (k n)"), w_raw[:, i % 4, :],
                               ACT.Copy, scale=w_scale[:, i:i + 1]).then_inc(w_hi_ready, 1)

            def weight_scaled_and_high(i, g):
                act.wait_ge(w_scale_ready, g + 1)
                act.activation(w_raw[:, i % 4, :], w_raw[:, i % 4, :], ACT.Copy, scale=w_scale[:, i:i + 1])\
                    .then_inc(w_scaled_ready, 1)
                act.wait_ge(w_scaled_ready, i - 2)
                act.activation(w_split[i][0][:, :, :].rearrange("p k n -> p (k n)"), w_raw[:, i % 4, :],
                               ACT.Copy).then_inc(w_hi_ready, 1)

            def gnn_qk_high(k):
                high(gnn_qk[0][:, k, :], S[k][:, :], qk_psum, k + 1, qk_hi_ready, scale=FOLD)

            weight_high(0, 0)
            gnn_qk_high(0)
            for i in range(2):
                high(xn_t[0][0][:, 2 * i:2 * i + 2, :].rearrange("p k n -> p (k n)"), ps_xt[i][:, :],
                     xt_psum, i + 1, xt_hi_ready)
            gnn_qk_high(1)
            weight_high(2, 1)
            gnn_qk_high(2)
            gnn_qk_high(3)

            def period(t, half, par, gnn, attn, tail, nxt):
                g, a, f = t, t - 1, t - 2
                if tail:
                    high(o_t[0][:, :, :].rearrange("p k n -> p (k n)"), ps_ot[:, :], ot_psum, f + 1, ot_hi_ready)
                if gnn:
                    high(xqk_t[0][:, 0:2, :].rearrange("p k n -> p (k n)"), ps_xqk[0][:, :],
                         xqk_psum, g * 2 + 1, xqk_hi_ready)
                if attn:
                    for c in range(TC):
                        act.wait_ge(xn2_ready, a * TC + c + 1)
                        act.activation(xn2_s[0][:, c, :], xn2[:, c, :], ACT.Copy).then_inc(xn2_hi_ready, 1)
                    act.wait_ge(z_ready, a * TC + TC)
                    act.activation(z_exp[:, :], z[:, :], ACT.Exp, scale=-1.0).then_inc(z_exp_ready, 1)
                if tail:
                    high(proj[0][:, :], ps_proj[:, :], proj_psum, f + 1, proj_hi_ready, scale=FOLD)
                if gnn:
                    high(xqk_t[0][:, 2:4, :].rearrange("p k n -> p (k n)"), ps_xqk[1][:, :],
                         xqk_psum, g * 2 + 2, xqk_hi_ready)
                if attn:
                    if tail:
                        act.wait_ge(out_psum, f * TC + TC)
                    high(pick_t[:, :], ps_pick_t, pick_psum, a + 1, pick_t_ready)
                    high(sel_t[0][:, :, :].rearrange("p k n -> p (k n)"), ps_sel[0][:, :],
                         sel_psum, a * 2 + 1, sel_hi_ready)
                    high(q_t[0][:, :, :].rearrange("p k n -> p (k n)"), ps_q[:, :], q_psum, a + 1, q_hi_ready)
                    high(k_t[0][:, :, :].rearrange("p k n -> p (k n)"), ps_k[:, :], k_psum, a + 1, k_hi_ready)
                if nxt:
                    for i in range(2):
                        high(xn_t[1 - par][0][:, 2 * i:2 * i + 2, :].rearrange("p k n -> p (k n)"), ps_xt[i][:, :],
                             xt_psum, (g + 1) * 2 + i + 1, xt_hi_ready)
                if gnn:
                    act.wait_ge(al_bias_ready, g + 1)
                    for c in range(TC):
                        act.activation(al_exp[:, c, :], al_relu[:, c, :], ACT.Exp, bias=al_bias[:, c:c + 1],
                                       scale=unscale_alpha, accum_out=al_sum[:, c:c + 1]).then_inc(al_exp_ready, 1)

                def exponentials(i):
                    act.wait_ge(s_bias_ready, a * GROUPS + i + 1)
                    for j in range(KC):
                        h = 4 * i + j
                        last = act.activation(e[:, i, j, :], ps_scores[i][:, j * P:j * P + P], ACT.Exp,
                                              bias=s_bias[:, h:h + 1], scale=unscale_scores)
                    last.then_inc(e_ready, 1)

                def y_high(c):
                    high(y[0][:, c, :], ps_y[c][:, :], y_psum, g * TC + c + 1, y_hi_ready)

                if attn:
                    exponentials(0)
                    exponentials(1)
                    high(v[0][:, :, 0:DH], ps_v[:, :].rearrange("p (h d) -> p h d", d=DH),
                         v_psum, a + 1, v_hi_ready)
                    exponentials(2)
                if gnn:
                    y_high(0)
                if attn:
                    exponentials(3)
                if gnn:
                    y_high(1)
                if first(t):
                    for i in (3, 4):
                        weight_scaled_and_high(i, 2)
                if first(t):
                    for i in (5, 6):
                        weight_scaled_and_high(i, 3)
                if attn:
                    for i in range(GROUPS):
                        high(e_t[0][:, i, :, :].rearrange("p k n -> p (k n)"), ps_et[i][:, :],
                             et_psum, a * GROUPS + i + 1, et_hi_ready)

            periods(act, period)

        @block.vector
        def _(dve):
            def low(dst, src, hi, hi_sem, count, done, scale=None):
                dve.wait_ge(hi_sem, count)
                if scale is None:
                    ins = dve.tensor_tensor(dst, src, hi, ALU.subtract)
                else:
                    ins = dve.scalar_tensor_tensor(out=dst, in0=src, scalar=scale, in1=hi,
                                                   op0=ALU.mult, op1=ALU.subtract)
                ins.then_inc(done, 1)

            def weight_maximum(i):
                dve.wait_ge(w_loaded[i], 16)
                last = dve.tensor_reduce(w_max[:, i:i + 1], w_raw[:, i % 4, :], AX.X, ALU.max,
                                         apply_absolute_value=True)
                if any(i == up - 1 for _, up in WGROUPS):
                    last.then_inc(w_max_ready, 1)

            def weight_scales(g):
                lo, up = WGROUPS[g]
                n = up - lo
                dve.wait_ge(w_top_psum, g + 1)
                dve.tensor_reduce(w_top[0:n, g:g + 1], ps_bound[g][0:n, 0:P], AX.X, ALU.max)\
                    .then_inc(w_top_ready, 1)
                dve.wait_ge(w_top_ready, g + 1)
                dve.tensor_scalar(w_diag[0:n, g, 0:n], ident[0:n, 0:n], w_top[0:n, g:g + 1], None, ALU.mult)\
                    .then_inc(w_diag_ready, 1)
                dve.wait_ge(w_bound_psum, g + 1)
                dve.tensor_scalar(w_bound[:, lo:up], ps_bound[g][:, P:P + n], 1e-30, None, ALU.max)\
                    .then_inc(w_bound_ready, 1)
                dve.wait_ge(w_bound_ready, g + 1)
                dve.tensor_scalar(w_pow[:, lo:up].bitcast(i32), w_bound[:, lo:up].bitcast(i32), 0x7F800000, None,
                                  ALU.bitwise_and).then_inc(w_pow_ready, 1)
                dve.wait_ge(w_pow_ready, g + 1)
                dve.reciprocal(w_rec[:, lo:up], w_pow[:, lo:up]).then_inc(w_rec_ready, 1)
                dve.wait_ge(w_rec_ready, g + 1)
                dve.tensor_scalar(w_scale[:, lo:up], w_rec[:, lo:up], 32.0, None, ALU.mult)\
                    .then_inc(w_scale_ready, 1)

            def weight_low(i, hi_sem, count):
                low(w_split[i][1][:, :, :].rearrange("p k n -> p (k n)"), w_raw[:, i % 4, :],
                    w_split[i][0][:, :, :].rearrange("p k n -> p (k n)"), hi_sem, count, w_lo_ready,
                    scale=w_scale[:, i:i + 1])

            def gnn_qk_low(k):
                low(gnn_qk[1][:, k, :], S[k][:, :], gnn_qk[0][:, k, :], qk_hi_ready, k + 1, qk_lo_ready, scale=FOLD)

            def statistics_of(n, c, src, stats_ready):
                dve.bn_stats(stats[n][:, c, :], src[:, c, :]).then_inc(stats_ready, 1)

            def moments_of(n, moments_ready):
                dve.drain()
                for c in range(TC):
                    dve.bn_aggr(moments[n][:, c, :], stats[n][:, c, :]).then_inc(moments_ready, 1)

            def normalise(n, dst, src, b, rstd_ready, done):
                dve.wait_ge(rstd_ready, b + 1)
                for c in range(TC):
                    dve.tensor_scalar(dst[:, c, :], src[:, c, :], moments[n][:, c, 0:1], rstd[n][:, c:c + 1],
                                      ALU.subtract, ALU.mult).then_inc(done, 1)

            def xt_low(b, buf):
                for i in range(2):
                    low(xn_t[buf][1][:, 2 * i:2 * i + 2, :].rearrange("p k n -> p (k n)"), ps_xt[i][:, :],
                        xn_t[buf][0][:, 2 * i:2 * i + 2, :].rearrange("p k n -> p (k n)"),
                        xt_hi_ready, b * 2 + i + 1, xt_lo_ready)

            dve.wait_ge(consts_ready, 5)
            weight_maximum(0)
            weight_maximum(1)
            weight_scales(0)
            dve.wait_ge(w_scale_ready, 1)
            dve.tensor_scalar(w_split[1][0][:, :, :].rearrange("p k n -> p (k n)"), w_raw[:, 1, :],
                              w_scale[:, 1:2], None, ALU.mult).then_inc(w1_hi_ready, 1)
            weight_low(0, w_hi_ready, 1)
            weight_low(1, w1_hi_ready, 1)
            dve.scalar_tensor_tensor(out=unscale[:, 1:2], in0=w_pow[:, 0:1], scalar=1.0 / (1024.0 * FOLD),
                                     in1=w_pow[:, 1:2], op0=ALU.mult, op1=ALU.mult).then_inc(unscale_ready, 1)
            dve.wait_ge(x_loaded[0], 16)
            for c in range(TC):
                statistics_of(0, c, x_in[0], stats1_ready)
            moments_of(0, moments1_ready)
            normalise(0, xn, x_in[0], 0, rstd1_ready, xn_ready)
            weight_maximum(2)
            gnn_qk_low(0)
            xt_low(0, 0)
            gnn_qk_low(1)
            weight_scales(1)
            dve.wait_ge(w_scale_ready, 2)
            dve.tensor_scalar(unscale[:, 2:3], w_pow[:, 2:3], 1.0 / 32.0, None, ALU.mult).then_inc(unscale_ready, 1)
            weight_low(2, w_hi_ready, 2)
            gnn_qk_low(2)
            gnn_qk_low(3)
            weight_maximum(3)

            def period(t, half, par, gnn, attn, tail, nxt):
                g, a, f = t, t - 1, t - 2
                buf_g, _ = slot(half, par, 0)
                buf_a, half_a = slot(half, par, 1)
                buf_f, _ = slot(half, par, 2)
                if attn:
                    if tail:
                        dve.wait_ge(out_stored[buf_a], half_a * 16)
                    for c in range(TC):
                        dve.wait_ge(msg_psum, a * TC + c + 1)
                        dve.scalar_tensor_tensor(out=x_mid[buf_a][:, c, :], in0=ps_msg[c][:, :], scalar=unscale_w,
                                                 in1=x_in[buf_a][:, c, :], op0=ALU.mult, op1=ALU.add)\
                            .then_inc(x_mid_ready, 1)
                if tail:
                    for i in range(2):
                        dve.wait_ge(o_psum, f * 2 + i + 1)
                        dve.reciprocal(o_rec[:, 8 * i:8 * i + 8],
                                       ps_o[i][:, 0:8 * (DH + 1)].rearrange("p (h d) -> p h d", d=DH + 1)[:, :, DH])\
                            .then_inc(o_rec_ready, 1)
                    for i in range(2):
                        dve.wait_ge(o_rec_ready, f * 2 + i + 1)
                        dve.tensor_tensor(
                            o_norm[:, 8 * i:8 * i + 8, :],
                            ps_o[i][:, 0:8 * (DH + 1)].rearrange("p (h d) -> p h d", d=DH + 1)[:, :, 0:DH],
                            o_rec[:, 8 * i:8 * i + 8].unsqueeze(2).to_broadcast([P, 8, DH]),
                            ALU.mult).then_inc(o_norm_ready, 1)
                if attn:
                    dve.wait_ge(x_mid_ready, a * TC + TC)
                    for c in range(TC):
                        statistics_of(1, c, x_mid[buf_a], stats2_ready)
                    moments_of(1, moments2_ready)
                if tail:
                    low(o_t[1][:, :, :].rearrange("p k n -> p (k n)"), ps_ot[:, :],
                        o_t[0][:, :, :].rearrange("p k n -> p (k n)"), ot_hi_ready, f + 1, ot_lo_ready)
                if attn:
                    normalise(1, xn2, x_mid[buf_a], a, rstd2_ready, xn2_ready)
                    for c in range(TC):
                        dve.wait_ge(xn2_ready, a * TC + c + 1)
                        dve.scalar_tensor_tensor(out=z_junk[:, c, :], in0=xn2[:, c, :], scalar=1.0,
                                                 in1=gate_row[:, :], op0=ALU.mult, op1=ALU.mult,
                                                 accum_out=z[:, c:c + 1]).then_inc(z_ready, 1)
                if gnn:
                    low(xqk_t[1][:, 0:2, :].rearrange("p k n -> p (k n)"), ps_xqk[0][:, :],
                        xqk_t[0][:, 0:2, :].rearrange("p k n -> p (k n)"), xqk_hi_ready, g * 2 + 1, xqk_lo_ready)
                if attn:
                    dve.wait_ge(z_psum, a + 1)
                    for c in range(TC):
                        dve.scalar_tensor_tensor(out=cmp_junk[:, c, :], in0=ps_z[:, 0:TOKENS], scalar=z[:, c:c + 1],
                                                 in1=tie[:, c, :], op0=ALU.subtract, op1=ALU.is_gt,
                                                 accum_out=rank[:, c:c + 1]).then_inc(rank_ready, 1)
                    for c in range(TC):
                        dve.wait_ge(rank_ready, a * TC + c + 1)
                        dve.tensor_scalar(pick[:, c, :], rank_row[:, :], rank[:, c:c + 1], None, ALU.is_equal)\
                            .then_inc(pick_ready, 1)
                if tail:
                    low(proj[1][:, :], ps_proj[:, :], proj[0][:, :], proj_hi_ready, f + 1, proj_lo_ready, scale=FOLD)
                if first(t):
                    weight_maximum(4)
                if gnn:
                    low(xqk_t[1][:, 2:4, :].rearrange("p k n -> p (k n)"), ps_xqk[1][:, :],
                        xqk_t[0][:, 2:4, :].rearrange("p k n -> p (k n)"), xqk_hi_ready, g * 2 + 2, xqk_lo_ready)
                if attn:
                    dve.wait_ge(z_exp_ready, a + 1)
                    dve.tensor_scalar(z_den[:, :], z_exp[:, :], 1.0, None, ALU.add).then_inc(z_den_ready, 1)
                    dve.wait_ge(sel_psum, a * 2 + 2)
                    dve.tensor_copy(sel_t[1][:, :, :].rearrange("p k n -> p (k n)"), ps_sel[1][:, :])\
                        .then_inc(sel_lo_ready, 1)
                    dve.wait_ge(z_den_ready, a + 1)
                    dve.reciprocal(gate[:, :], z_den[:, :]).then_inc(gate_ready, 1)
                    dve.wait_ge(gate_ready, a + 1)
                    dve.tensor_scalar(gate_out[buf_a][:, :], gate[:, :], unscale_out, None, ALU.mult)\
                        .then_inc(gate_out_ready, 1)
                if tail:
                    for c in range(TC):
                        dve.wait_ge(out_psum, f * TC + c + 1)
                        dve.scalar_tensor_tensor(out=x_mid[buf_f][:, c, :], in0=ps_out[c][:, :],
                                                 scalar=gate_out[buf_f][:, c:c + 1], in1=x_mid[buf_f][:, c, :],
                                                 op0=ALU.mult, op1=ALU.add).then_inc(out_ready, 1)
                if nxt:
                    buf_n, half_n = slot(half, par, -1)
                    dve.wait_ge(x_loaded[buf_n], half_n * 16 + 16)
                    for c in range(TC):
                        statistics_of(0, c, x_in[buf_n], stats1_ready)
                    moments_of(0, moments1_ready)
                    normalise(0, xn, x_in[buf_n], g + 1, rstd1_ready, xn_ready)
                if attn:
                    low(q_t[1][:, :, :].rearrange("p k n -> p (k n)"), ps_q[:, :],
                        q_t[0][:, :, :].rearrange("p k n -> p (k n)"), q_hi_ready, a + 1, q_lo_ready)
                    low(k_t[1][:, :, :].rearrange("p k n -> p (k n)"), ps_k[:, :],
                        k_t[0][:, :, :].rearrange("p k n -> p (k n)"), k_hi_ready, a + 1, k_lo_ready)
                if gnn:
                    dve.wait_ge(alpha_psum, g + 1)
                    dve.wait_ge(adj_loaded[buf_g], half * 16 + 16)
                    dve.scalar_tensor_tensor(out=al_masked[:, :, :].rearrange("p c n -> p (c n)"),
                                             in0=adj_in[buf_g][:, :, :].rearrange("p c n -> p (c n)"), scalar=0.0,
                                             in1=ps_alpha[:, :], op0=ALU.not_equal, op1=ALU.mult)\
                        .then_inc(al_masked_ready, 1)
                    dve.wait_ge(al_masked_ready, g + 1)
                    for c in range(TC):
                        dve.tensor_scalar(al_relu[:, c, :], al_masked[:, c, :], 0.0, None, ALU.max, ALU.max,
                                          accum_out=al_max[:, c:c + 1]).then_inc(al_relu_ready, 1)
                    dve.wait_ge(al_relu_ready, g * TC + TC)
                    dve.tensor_scalar(al_bias[:, :], al_max[:, :], unscale_alpha, -1.0, ALU.mult, ALU.mult)\
                        .then_inc(al_bias_ready, 1)
                if nxt:
                    xt_low(g + 1, 1 - par)
                if attn:
                    dve.wait_ge(scores_psum, a + 1)
                    for i in range(GROUPS):
                        dve.tensor_reduce(s_max[:, 4 * i:4 * i + 4],
                                          ps_scores[i][:, :].rearrange("p (j n) -> p j n", n=P), AX.X, ALU.max)\
                            .then_inc(s_max_ready, 1)
                        dve.wait_ge(s_max_ready, a * GROUPS + i + 1)
                        dve.tensor_scalar(s_bias[:, 4 * i:4 * i + 4], s_max[:, 4 * i:4 * i + 4], unscale_scores, -1.0,
                                          ALU.mult, ALU.mult).then_inc(s_bias_ready, 1)
                if gnn:
                    dve.wait_ge(al_exp_ready, g * TC + TC)
                    dve.reciprocal(al_rec[:, :], al_sum[:, :]).then_inc(al_rec_ready, 1)
                    dve.wait_ge(al_rec_ready, g + 1)
                    for c in range(TC):
                        dve.tensor_scalar(alpha[0][:, c, :], al_exp[:, c, :], al_rec[:, c:c + 1], None, ALU.mult)\
                            .then_inc(alpha_hi_ready, 1)
                    for c in range(TC):
                        low(alpha[1][:, c, :], al_exp[:, c, :], alpha[0][:, c, :], alpha_hi_ready,
                            g * TC + c + 1, alpha_lo_ready, scale=al_rec[:, c:c + 1])
                if attn:
                    low(v[1][:, :, 0:DH], ps_v[:, :].rearrange("p (h d) -> p h d", d=DH), v[0][:, :, 0:DH],
                        v_hi_ready, a + 1, v_lo_ready)
                if gnn:
                    for c in range(TC):
                        low(y[1][:, c, :], ps_y[c][:, :], y[0][:, c, :], y_hi_ready, g * TC + c + 1, y_lo_ready)
                if first(t):
                    weight_scales(2)
                if first(t):
                    weight_maximum(5)
                    weight_maximum(6)
                    weight_scales(3)
                    dve.scalar_tensor_tensor(out=unscale[:, 4:5], in0=w_pow[:, 3:4],
                                             scalar=1.0 / (1024.0 * math.sqrt(DH)), in1=w_pow[:, 4:5],
                                             op0=ALU.mult, op1=ALU.mult).then_inc(unscale_ready, 1)
                    dve.wait_ge(w_scale_ready, 4)
                    dve.scalar_tensor_tensor(out=unscale[:, 6:7], in0=w_pow[:, 5:6], scalar=1.0 / (1024.0 * FOLD),
                                             in1=w_pow[:, 6:7], op0=ALU.mult, op1=ALU.mult).then_inc(unscale_ready, 1)
                    dve.wait_ge(unscale_ready, 4)
                if attn:
                    for i in range(GROUPS):
                        low(e_t[1][:, i, :, :].rearrange("p k n -> p (k n)"), ps_et[i][:, :],
                            e_t[0][:, i, :, :].rearrange("p k n -> p (k n)"), et_hi_ready,
                            a * GROUPS + i + 1, et_lo_ready)

            dve.wait_ge(unscale_ready, 2)
            dve.wait_ge(gate_row_loaded, 16)
            periods(dve, period)

        @block.tensor
        def _(pe):
            PASSES = ((0, 0), (0, 1), (1, 0))

            def product(dst, steps, lhs, rhs, passes=range(3)):
                for n in passes:
                    l, r = PASSES[n]
                    for k in range(steps):
                        last = pe.matmul(dst, lhs(l, k), rhs(r, k), start=(n == 0 and k == 0),
                                         stop=(n == 2 and k == steps - 1))
                return last

            def weight_bounds(g):
                lo, up = WGROUPS[g]
                n = up - lo
                pe.wait_ge(w_max_ready, g + 1)
                pe.transpose(ps_bound[g][0:n, 0:P], w_max[:, lo:up], ident[:, :]).then_inc(w_top_psum, 1)
                pe.wait_ge(w_diag_ready, g + 1)
                pe.matmul(ps_bound[g][:, P:P + n], ones[0:n, :], w_diag[0:n, g, 0:n], start=True, stop=True)\
                    .then_inc(w_bound_psum, 1)

            def transpose_x(b):
                pe.wait_ge(xn_ready, b * TC + TC)
                for i in range(2):
                    for k in (2 * i, 2 * i + 1):
                        for c in range(TC):
                            at = (k % 2) * TOKENS + c * P
                            last = pe.transpose(ps_xt[i][:, at:at + P], xn[:, c, k * P:k * P + P], ident[:, :])
                    last.then_inc(xt_psum, 1)

            pe.wait_ge(consts_ready, 5)
            weight_bounds(0)

            def gnn_qk_product(k, passes):
                return product(S[k][:, :], KC, lambda p, o: w_split[0][p][:, o, k * P:k * P + P],
                               lambda p, o: w_split[1][p][:, o, :], passes)

            pe.wait_ge(w_hi_ready, 1)
            pe.wait_ge(w1_hi_ready, 1)
            for k in range(KC):
                gnn_qk_product(k, range(1))
            pe.wait_ge(w_lo_ready, 2)
            for k in range(KC):
                gnn_qk_product(k, range(1, 3)).then_inc(qk_psum, 1)
                if k == 0:
                    transpose_x(0)
                if k == 1:
                    weight_bounds(1)
            pe.wait_ge(qk_lo_ready, KC)

            def head_scores(tiles, groups):
                for j in tiles:
                    for n, (l, r) in enumerate(PASSES):
                        for i in groups:
                            rows = slice(i * DH, i * DH + DH)
                            last = pe.matmul(ps_scores[i][:, j * P:j * P + P], q_t[l][rows, j, :], k_t[r][rows, j, :],
                                             start=(n == 0), stop=(n == 2))
                return last

            def project(passes):
                return product(ps_proj[:, :], KC, lambda p, k: o_t[p][:, k, :],
                               lambda p, k: w_split[6][p][:, k, :], passes)

            def period(t, half, par, gnn, attn, tail, nxt):
                g, a, f = t, t - 1, t - 2
                x_t = xn_t[par]

                def xqk(j):
                    return product(ps_xqk[j // 2][:, (j % 2) * TOKENS:(j % 2 + 1) * TOKENS], KC,
                                   lambda p, k: gnn_qk[p][:, k, j * P:j * P + P], lambda p, k: x_t[p][:, k, :])

                def scores_t(m):
                    return product(ps_alpha[:, m * TOKENS:(m + 1) * TOKENS], KC,
                                   lambda p, k: x_t[p][:, k, m * P:m * P + P], lambda p, k: xqk_t[p][:, k, :])

                if gnn:
                    pe.wait_ge(xt_lo_ready, g * 2 + 2)
                    xqk(0)
                if tail:
                    pe.wait_ge(o_norm_ready, f * 2 + 2)
                    for k in range(KC):
                        last = pe.transpose(ps_ot[:, k * P:k * P + P],
                                            o_norm[:, :, :].rearrange("p h d -> p (h d)")[:, k * P:k * P + P],
                                            ident[:, :])
                    last.then_inc(ot_psum, 1)
                if gnn:
                    xqk(1).then_inc(xqk_psum, 1)
                    xqk(2)
                if tail:
                    pe.wait_ge(ot_lo_ready, f + 1)
                    project(range(2))
                if attn:
                    pe.wait_ge(z_ready, a * TC + TC)
                    for c in range(TC):
                        last = pe.transpose(ps_z[:, c * P:c * P + P], z[:, c:c + 1].to_broadcast([P, P]), ident[:, :])
                    last.then_inc(z_psum, 1)
                if tail:
                    project((2,)).then_inc(proj_psum, 1)
                if gnn:
                    xqk(3).then_inc(xqk_psum, 1)
                def pick_part(p):
                    for k in range(KC):
                        for c in range(TC):
                            last = pe.matmul(ps_sel[p][:, k * P:k * P + P], xn2_s[p][:, c, k * P:k * P + P],
                                             pick[:, c, :], start=(c == 0), stop=(c == TC - 1))
                    last.then_inc(sel_psum, 1)

                if attn:
                    pe.wait_ge(pick_ready, a * TC + TC)
                    for c in range(TC):
                        last = pe.transpose(ps_pick_t[:, c * P:c * P + P], pick[:, c, :], ident16[:, :])
                    last.then_inc(pick_psum, 1)
                    pe.wait_ge(xn2_hi_ready, a * TC + TC)
                    pick_part(0)
                if tail:
                    pe.wait_ge(proj_lo_ready, f + 1)
                    for c in range(TC):
                        for p in range(2):
                            last = pe.matmul(ps_out[c][:, :], pick_t[:, c * P:c * P + P], proj[p][:, :],
                                             start=(p == 0), stop=(p == 1))
                        last.then_inc(out_psum, 1)
                if attn:
                    pe.wait_ge(xn2_lo_ready, a * TC + TC)
                    pick_part(1)
                if gnn:
                    pe.wait_ge(xqk_lo_ready, g * 2 + 2)
                    scores_t(0)
                if attn:
                    pe.wait_ge(sel_hi_ready, a + 1)
                    pe.wait_ge(sel_lo_ready, a + 1)
                    for w, ps, done in ((3, ps_q, q_psum), (4, ps_k, k_psum)):
                        if second(t):
                            pe.wait_ge(w_low_by_pool, w - 2)
                        for j in range(KC):
                            last = product(ps[:, j * P:j * P + P], KC, lambda p, k: w_split[w][p][:, k, j * P:j * P + P],
                                           lambda p, k: sel_t[p][:, k, :])
                        last.then_inc(done, 1)
                if gnn:
                    scores_t(1).then_inc(alpha_psum, 1)
                if nxt:
                    if tail:
                        pe.wait_ge(out_ready, f * TC + TC)
                    transpose_x(g + 1)
                if attn:
                    pe.wait_ge(q_lo_ready, a + 1)
                    pe.wait_ge(k_lo_ready, a + 1)
                    pe.wait_ge(pick_t_ready, a + 1)
                    head_scores(range(2), range(GROUPS - 1))
                    if gnn:
                        pe.wait_ge(al_masked_ready, g + 1)
                    head_scores(range(2), (GROUPS - 1,))
                    last = head_scores(range(2, KC), range(GROUPS))
                    last.then_inc(scores_psum, 1)
                    if nxt:
                        pe.wait_ge(xt_lo_ready, (g + 1) * 2 + 1)
                    elif tail:
                        pe.wait_ge(out_ready, f * TC + TC)
                    if second(t):
                        pe.wait_ge(w_low_by_pool, 3)
                    product(ps_v[:, :], KC, lambda p, k: sel_t[p][:, k, :], lambda p, k: w_split[5][p][:, k, :])\
                        .then_inc(v_psum, 1)
                if gnn:
                    if first(t):
                        pe.wait_ge(w_lo_ready, 3)
                    if nxt:
                        pe.wait_ge(xt_lo_ready, (g + 1) * 2 + 2)
                    for m in range(TC):
                        product(ps_y[m][:, :], KC, lambda p, k: x_t[p][:, k, m * P:m * P + P],
                                lambda p, k: w_split[2][p][:, k, :]).then_inc(y_psum, 1)
                if first(t):
                    weight_bounds(2)
                if attn:
                    for i in range(GROUPS):
                        pe.wait_ge(e_ready, a * GROUPS + i + 1)
                        for j in range(KC):
                            last = pe.transpose(ps_et[i][:, j * P:j * P + P], e[:, i, j, :], ident[:, :])
                        last.then_inc(et_psum, 1)
                if gnn:
                    pe.wait_ge(y_lo_ready, g * TC + TC)
                    pe.wait_ge(alpha_lo_ready, g * TC + TC)
                    for c in range(TC):
                        product(ps_msg[c][:, :], TC, lambda p, m: alpha[p][:, m, c * P:c * P + P],
                                lambda p, m: y[p][:, m, :]).then_inc(msg_psum, 1)
                if first(t):
                    weight_bounds(3)
                if attn:
                    pe.wait_ge(et_lo_ready, a * GROUPS + GROUPS)
                    pe.wait_ge(v_lo_ready, a + 1)
                    for i in range(2):
                        for h in range(8 * i, 8 * i + 8):
                            at = (h - 8 * i) * (DH + 1)
                            last = product(ps_o[i][:, at:at + DH + 1], 1,
                                           lambda p, k: e_t[p][:, h % GROUPS, h // GROUPS, :],
                                           lambda p, k: v[p][:, h, :])
                        last.then_inc(o_psum, 1)
                if second(t):
                    pe.wait_ge(w_low_by_pool, 4)

            periods(pe, period)


_NAMES = ["x", "adj_t", "gnn_w", "gnn_wq_t", "gnn_wk_t", "gate_w", "wq", "wk", "wv", "wo"]


def kernel(x, adj, L0_gnn_weight, L0_gnn_wq, L0_gnn_wk, L0_ffn_Wg, L0_ffn_Wq, L0_ffn_Wk, L0_ffn_Wv, L0_ffn_Wo):
    import numpy as _np
    import concourse.bacc as _bacc
    from concourse import mybir as _mybir
    from concourse.bass_utils import run_bass_kernel_spmd as _run

    given = [
        _np.asarray(x), _np.asarray(adj).transpose(0, 2, 1), _np.asarray(L0_gnn_weight),
        _np.asarray(L0_gnn_wq).T, _np.asarray(L0_gnn_wk).T, _np.asarray(L0_ffn_Wg).reshape(-1),
        _np.asarray(L0_ffn_Wq), _np.asarray(L0_ffn_Wk), _np.asarray(L0_ffn_Wv), _np.asarray(L0_ffn_Wo),
    ]
    nc = _bacc.Bacc("TRN2", target_bir_lowering=False, num_devices=1)
    arrays, args = {}, []
    for name, a in zip(_NAMES, given):
        a = _np.ascontiguousarray(a)
        arrays[f"in_{name}"] = a
        args.append(nc.dram_tensor(f"in_{name}", a.shape, _mybir.dt.from_np(a.dtype), kind="ExternalInput").ap())
    args.append(nc.dram_tensor("out_0", given[0].shape, _mybir.dt.float32, kind="ExternalOutput").ap())
    gnn_then_routed_attention(nc, *args)
    result = _run(nc, [arrays], core_ids=[0])
    return result.results[0]["out_0"]
```

```python
import math
from contextlib import ExitStack

import concourse.bass as bass
from concourse import mybir


def gnn_then_routed_attention(nc, x, adj_t, gnn_w, gnn_wq_t, gnn_wk_t, gate_w, wq, wk, wv, wo, out):
    fp32, fp16, i32 = mybir.dt.float32, mybir.dt.float16, mybir.dt.int32
    ALU, ACT, AX = mybir.AluOpType, mybir.ActivationFunctionType, mybir.AxisListType

    BATCHES, TOKENS, DIM = x.shape
    P = 128
    TC = TOKENS // P
    KC = DIM // P
    PICKED = TOKENS // 2
    HEADS = 16
    DH = DIM // HEADS
    GROUPS = P // DH
    EPS = 1e-5
    TINY = 2.0 ** -126
    FOLD = 2.0 ** -15
    assert PICKED == P and TC == 2 and KC == 4 and GROUPS == KC

    ctx = ExitStack()
    with ctx:
        def sb(name, shape, dt=fp32):
            return ctx.enter_context(nc.sbuf_tensor(name, shape, dt))

        def sem(name):
            return ctx.enter_context(nc.semaphore(name))

        def pair(name, shape):
            return [sb(f"{name}_hi", shape, fp16), sb(f"{name}_lo", shape, fp16)]

        NW = 7
        W_SLOTS = 5
        w_raw = sb("w_raw", [P, W_SLOTS, KC * DIM])
        w_split = [pair(f"w{i}", [P, KC, DIM]) for i in range(NW)]
        gnn_qk = pair("gnn_qk", [P, KC, DIM])
        w_max = sb("w_max", [P, NW])
        w_top = sb("w_top", [3, 4])
        w_diag = sb("w_diag", [3, 4, 3])
        w_bound = sb("w_bound", [P, NW])
        w_pow = sb("w_pow", [P, NW])
        w_rec = sb("w_rec", [P, NW])
        w_scale = sb("w_scale", [P, NW])
        unscale = sb("unscale", [P, 8])
        unscale_alpha = unscale[:, 1:2]
        unscale_w = unscale[:, 2:3]
        unscale_scores = unscale[:, 4:5]
        unscale_out = unscale[:, 6:7]
        gate_row = sb("gate_row", [P, DIM])
        ident = sb("ident", [P, P])
        ones = sb("ones", [P, P])
        rank_row = sb("rank_row", [P, P])
        tie = sb("tie", [P, TC, TOKENS])
        half_neg = sb("half_neg", [P, TC])
        eps = sb("eps", [P, TC])

        x_in = [sb(f"x_in{i}", [P, TC, DIM]) for i in range(2)]
        adj_in = [sb(f"adj_in{i}", [P, TC, TOKENS], i32) for i in range(2)]
        x_mid = [sb(f"x_mid{i}", [P, TC, DIM]) for i in range(2)]
        stats = [sb(f"stats{i}", [P, TC, 6]) for i in range(2)]
        moments = [sb(f"moments{i}", [P, TC, 2]) for i in range(2)]
        var_eps = [sb(f"var_eps{i}", [P, TC]) for i in range(2)]
        rstd = [sb(f"rstd{i}", [P, TC]) for i in range(2)]
        xn = sb("xn", [P, TC, DIM])
        xn_t = [pair(f"xn_t{i}", [P, KC, TOKENS]) for i in range(2)]
        xqk_t = pair("xqk_t", [P, KC, TOKENS])
        al_masked = sb("al_masked", [P, TC, TOKENS])
        al_relu = sb("al_relu", [P, TC, TOKENS])
        al_max = sb("al_max", [P, TC])
        al_bias = sb("al_bias", [P, TC])
        al_exp = sb("al_exp", [P, TC, TOKENS])
        al_sum = sb("al_sum", [P, TC])
        al_rec = sb("al_rec", [P, TC])
        alpha = pair("alpha", [P, TC, TOKENS])
        y = pair("y", [P, TC, DIM])
        xn2 = sb("xn2", [P, TC, DIM])
        xn2_s = pair("xn2_s", [P, TC, DIM])
        z_junk = sb("z_junk", [P, TC, DIM], fp16)
        z = sb("z", [P, TC])
        z_near = sb("z_near", [P, TC])
        z_id = sb("z_id", [P, 2, TC, 2], fp16)
        z_exp = sb("z_exp", [P, 1])
        z_den = sb("z_den", [P, 1])
        gate = sb("gate", [P, 1])
        gate_out = [sb(f"gate_out{i}", [P, 1]) for i in range(2)]
        picked_id = [sb(f"picked_id{i}", [P, 1], i32) for i in range(2)]
        first_row = sb("first_row", [P, 1], i32)
        batch_rows = sb("batch_rows", [P, 1], i32)
        picked_row = [sb(f"picked_row{i}", [P, 1], i32) for i in range(2)]
        cmp_junk = sb("cmp_junk", [P, TC, TOKENS], fp16)
        rank = sb("rank", [P, TC])
        pick = sb("pick", [P, TC, PICKED], fp16)
        sel_t = pair("sel_t", [P, KC, PICKED])
        q_t = pair("q_t", [P, KC, PICKED])
        k_t = pair("k_t", [P, KC, PICKED])
        v = sb("v", [P, HEADS, 2, DH], fp16)
        s_max = sb("s_max", [P, HEADS])
        s_bias = sb("s_bias", [P, HEADS])
        e = sb("e", [P, GROUPS, KC, PICKED])
        e_t = pair("e_t", [P, GROUPS, KC, PICKED])
        e_sum = sb("e_sum", [P, HEADS])
        o_rec = sb("o_rec", [P, HEADS])
        o_cross = sb("o_cross", [P, HEADS, DH])
        o_sum = sb("o_sum", [P, HEADS, DH])
        o_norm = sb("o_norm", [P, HEADS, DH])
        o_t = pair("o_t", [P, KC, PICKED])
        gated = [sb(f"gated{i}", [P, DIM]) for i in range(2)]

        banks = [ctx.enter_context(nc.psum_tensor(f"bank{i}", [P, DIM], fp32)) for i in range(8)]
        S, B = banks[:4], banks[4:]
        ps_xqk = [S[0], S[1]]
        ps_ot = S[2]
        ps_z = B[3]
        ps_picked = S[2][:, 0:2]
        ps_proj = S[3]
        ps_alpha = S[3]
        ps_scores = S
        ps_et = S
        ps_sel = [B[2], B[3]]
        ps_q, ps_k, ps_v = B[2], B[3], B[0]
        ps_y = [B[1], B[2]]
        ps_xt = [B[0], B[1]]
        ps_msg = [B[1], B[2]]
        ps_o = [B[3], B[0]]
        ps_bound = [B[2], B[2], S[2], B[2]]

        consts_zeroed = sem("consts_zeroed")
        consts_ready = sem("consts_ready")
        w_max_ready = sem("w_max_ready")
        w_top_psum = sem("w_top_psum")
        w_top_ready = sem("w_top_ready")
        w_diag_ready = sem("w_diag_ready")
        w_bound_psum = sem("w_bound_psum")
        w_bound_ready = sem("w_bound_ready")
        w_pow_ready = sem("w_pow_ready")
        w_rec_ready = sem("w_rec_ready")
        w_scale_ready = sem("w_scale_ready")
        w_hi_ready = sem("w_hi_ready")
        w_lo_ready = sem("w_lo_ready")
        w1_hi_ready = sem("w1_hi_ready")
        w_scaled_ready = sem("w_scaled_ready")
        w_scaled_by_pool = sem("w_scaled_by_pool")
        w_low_by_pool = sem("w_low_by_pool")
        qk_psum = sem("qk_psum")
        qk_hi_ready = sem("qk_hi_ready")
        qk_lo_ready = sem("qk_lo_ready")
        unscale_ready = sem("unscale_ready")
        stats1_ready = sem("stats1_ready")
        moments1_ready = sem("moments1_ready")
        var1_ready = sem("var1_ready")
        rstd1_ready = sem("rstd1_ready")
        xn_ready = sem("xn_ready")
        stats2_ready = sem("stats2_ready")
        moments2_ready = sem("moments2_ready")
        var2_ready = sem("var2_ready")
        rstd2_ready = sem("rstd2_ready")
        xn2_ready = sem("xn2_ready")
        xn2_hi_ready = sem("xn2_hi_ready")
        xn2_lo_ready = sem("xn2_lo_ready")
        xt_psum = sem("xt_psum")
        xt_hi_ready = sem("xt_hi_ready")
        xt_lo_ready = sem("xt_lo_ready")
        xqk_psum = sem("xqk_psum")
        xqk_hi_ready = sem("xqk_hi_ready")
        xqk_lo_ready = sem("xqk_lo_ready")
        alpha_psum = sem("alpha_psum")
        al_masked_ready = sem("al_masked_ready")
        al_relu_ready = sem("al_relu_ready")
        al_bias_ready = sem("al_bias_ready")
        al_exp_ready = sem("al_exp_ready")
        al_rec_ready = sem("al_rec_ready")
        alpha_hi_ready = sem("alpha_hi_ready")
        alpha_lo_ready = sem("alpha_lo_ready")
        y_psum = sem("y_psum")
        y0_hi_ready = sem("y0_hi_ready")
        y1_hi_ready = sem("y1_hi_ready")
        y_lo_ready = sem("y_lo_ready")
        msg_psum = sem("msg_psum")
        x_mid_ready = sem("x_mid_ready")
        z_ready = sem("z_ready")
        z_exp_ready = sem("z_exp_ready")
        z_den_ready = sem("z_den_ready")
        gate_ready = sem("gate_ready")
        gate_out_ready = sem("gate_out_ready")
        picked_psum = sem("picked_psum")
        picked_id_ready = sem("picked_id_ready")
        z_near_ready = sem("z_near_ready")
        z_hi_ready = sem("z_hi_ready")
        z_lo_ready = sem("z_lo_ready")
        picked_row_ready = sem("picked_row_ready")
        gated_ready = sem("gated_ready")
        z_psum = sem("z_psum")
        rank_ready = sem("rank_ready")
        pick_ready = sem("pick_ready")
        sel_psum = sem("sel_psum")
        sel_hi_ready = sem("sel_hi_ready")
        sel_lo_ready = sem("sel_lo_ready")
        q_psum = sem("q_psum")
        q_hi_ready = sem("q_hi_ready")
        q_lo_ready = sem("q_lo_ready")
        k_psum = sem("k_psum")
        k_hi_ready = sem("k_hi_ready")
        k_lo_ready = sem("k_lo_ready")
        v_psum = sem("v_psum")
        v_hi_ready = sem("v_hi_ready")
        v_lo_ready = sem("v_lo_ready")
        scores_psum = sem("scores_psum")
        s_max_ready = sem("s_max_ready")
        s_bias_ready = sem("s_bias_ready")
        e_ready = sem("e_ready")
        et_psum = sem("et_psum")
        et_hi_ready = sem("et_hi_ready")
        et_lo_ready = sem("et_lo_ready")
        o_psum = sem("o_psum")
        o_rec_ready = sem("o_rec_ready")
        o_cross_ready = sem("o_cross_ready")
        o_sum_ready = sem("o_sum_ready")
        o_norm_ready = sem("o_norm_ready")
        ot_psum = sem("ot_psum")
        ot_hi_ready = sem("ot_hi_ready")
        ot_lo_ready = sem("ot_lo_ready")
        proj_psum = sem("proj_psum")
        gate_row_loaded = sem("gate_row_loaded")
        w_loaded = [sem(f"w{i}_loaded") for i in range(NW)]
        x_loaded = [sem(f"x_loaded{i}") for i in range(2)]
        adj_loaded = [sem(f"adj_loaded{i}") for i in range(2)]
        out_stored = [sem(f"out_stored{i}") for i in range(2)]
        gated_added = [sem(f"gated_added{i}") for i in range(2)]

        WGROUPS = [(0, 2), (2, 3), (3, 6), (6, NW)]

        x_view = x.rearrange("b (c p) d -> b p c d", p=P)
        adj_view = adj_t.rearrange("b (c p) n -> b p c n", p=P)
        out_view = out.rearrange("b (c p) d -> b p c d", p=P)
        out_rows = out.rearrange("b n d -> (b n) d")

        def periods(engine, period):
            period(0, 0, 0, gnn=True, attn=False, tail=False, nxt=True)
            period(1, 0, 1, gnn=True, attn=True, tail=False, nxt=True)
            period(2, 1, 0, gnn=True, attn=True, tail=True, nxt=True)
            period(3, 1, 1, gnn=True, attn=True, tail=True, nxt=True)
            with engine.Fori(2, BATCHES // 2 - 1) as half:
                period(half * 2, half, 0, gnn=True, attn=True, tail=True, nxt=True)
                period(half * 2 + 1, half, 1, gnn=True, attn=True, tail=True, nxt=True)
            end = BATCHES // 2
            period(BATCHES - 2, end - 1, 0, gnn=True, attn=True, tail=True, nxt=True)
            period(BATCHES - 1, end - 1, 1, gnn=True, attn=True, tail=True, nxt=False)
            period(BATCHES, end, 0, gnn=False, attn=True, tail=True, nxt=False)
            period(BATCHES + 1, end, 1, gnn=False, attn=False, tail=True, nxt=False)

        def first(t):
            return isinstance(t, int) and t == 0

        def second(t):
            return isinstance(t, int) and t == 1

        def reused(before):
            return not (isinstance(before, int) and before == 0)

        def slot(half, par, back):
            return (par - back) % 2, half + (par - back) // 2

        block = ctx.enter_context(nc.Block())

        @block.sync
        def _(sp):
            def load_x(b, buf):
                sp.dma_start(x_in[buf][:, :, :], x_view[b]).then_inc(x_loaded[buf], 16)

            def load_adj(b, buf):
                sp.dma_start(adj_in[buf][:, :, :], adj_view[b]).then_inc(adj_loaded[buf], 16)

            def load_w(i, w):
                sp.dma_start(w_raw[:, i % W_SLOTS, :].rearrange("p (k n) -> p k n", k=KC),
                             w.rearrange("(k p) n -> p k n", p=P)).then_inc(w_loaded[i], 16)

            load_w(0, gnn_wq_t)
            load_w(1, gnn_wk_t)
            load_x(0, 0)
            load_adj(0, 0)
            load_w(2, gnn_w)
            load_x(1, 1)
            load_adj(1, 1)
            sp.dma_start(gate_row[:, :], gate_w.partition_broadcast(P)).then_inc(gate_row_loaded, 16)
            for i, w in ((3, wq), (4, wk), (5, wv), (6, wo)):
                if i >= W_SLOTS:
                    sp.wait_ge(w_lo_ready, i - W_SLOTS + 1)
                load_w(i, w)

            def period(t, half, par, gnn, attn, tail, nxt):
                if nxt and attn:
                    sp.wait_ge(x_mid_ready, (t - 1) * TC + TC)
                    load_x(t + 1, slot(half, par, -1)[0])
                if attn:
                    sp.wait_ge(x_mid_ready, (t - 1) * TC + TC)
                    buf = slot(half, par, 1)[0]
                    sp.dma_start(out_view[t - 1], x_mid[buf][:, :, :]).then_inc(out_stored[buf], 16)
                if gnn and not (isinstance(t, int) and t + 2 >= BATCHES):
                    sp.wait_ge(al_masked_ready, t + 1)
                    load_adj(t + 2, slot(half, par, -2)[0])

            periods(sp, period)
            for buf in range(2):
                sp.wait_ge(out_stored[buf], 16 * (BATCHES // 2))
                sp.wait_ge(gated_added[buf], 16 * (BATCHES // 2))

        @block.gpsimd
        def _(pool):
            pool.memset(half_neg[:, :], -0.5).then_inc(consts_zeroed, 1)
            pool.memset(eps[:, :], EPS).then_inc(consts_zeroed, 1)
            pool.memset(ident[:, :], 0.0).then_inc(consts_zeroed, 1)
            pool.memset(tie[:, :, :], 0.0).then_inc(consts_zeroed, 1)
            pool.memset(first_row[:, :], 0).then_inc(consts_zeroed, 1)
            pool.memset(batch_rows[:, :], TOKENS).then_inc(consts_zeroed, 1)
            pool.memset(z_id[:, :, :, :], 0.0).then_inc(consts_zeroed, 1)
            pool.wait_ge(consts_zeroed, 7)
            pool.affine_select(out=ident[:, :], in_=ident[:, :], compare_op=ALU.not_equal, fill=1.0, base=0,
                               pattern=[[-1, P]], channel_multiplier=1).then_inc(consts_ready, 1)
            pool.memset(ones[:, :], 1.0).then_inc(consts_ready, 1)
            pool.iota(rank_row[:, :], pattern=[[1, P]], base=0, channel_multiplier=0,
                      allow_small_or_imprecise_dtypes=True).then_inc(consts_ready, 1)
            pool.affine_select(out=tie[:, :, :], in_=tie[:, :, :], compare_op=ALU.is_ge, fill=-TINY, base=0,
                               pattern=[[-P, TC], [1, TOKENS]], channel_multiplier=-1)\
                .then_inc(consts_ready, 1)
            pool.iota(z_id[:, 0, :, 1], pattern=[[P, TC]], base=0, channel_multiplier=1,
                      allow_small_or_imprecise_dtypes=True).then_inc(consts_ready, 1)

            def inverse_std(n, b, moments_ready, var_ready, rstd_ready):
                pool.wait_ge(moments_ready, b * TC + TC)
                pool.tensor_tensor(var_eps[n][:, :], moments[n][:, :, 1], eps[:, :], ALU.add)\
                    .then_inc(var_ready, 1)
                pool.wait_ge(var_ready, b + 1)
                pool.tensor_tensor(rstd[n][:, :], var_eps[n][:, :], half_neg[:, :], ALU.pow)\
                    .then_inc(rstd_ready, 1)

            def weight_low(i):
                pool.wait_ge(w_hi_ready, min(i + 1, NW))
                pool.tensor_tensor(w_split[i][1][:, :, :].rearrange("p k n -> p (k n)"), w_raw[:, i % W_SLOTS, :],
                                   w_split[i][0][:, :, :].rearrange("p k n -> p (k n)"), ALU.subtract)\
                    .then_inc(w_low_by_pool, 1)

            inverse_std(0, 0, moments1_ready, var1_ready, rstd1_ready)
            weight_low(2)

            def period(t, half, par, gnn, attn, tail, nxt):
                if tail:
                    for i in range(2):
                        pool.wait_ge(o_sum_ready, (t - 2) * 2 + i + 1)
                        pool.tensor_tensor(
                            o_norm[:, 8 * i:8 * i + 8, :], o_sum[:, 8 * i:8 * i + 8, :],
                            o_rec[:, 8 * i:8 * i + 8].unsqueeze(2).to_broadcast([P, 8, DH]),
                            ALU.mult).then_inc(o_norm_ready, 1)
                if attn:
                    inverse_std(1, t - 1, moments2_ready, var2_ready, rstd2_ready)
                    for c in range(TC):
                        pool.wait_ge(xn2_hi_ready, (t - 1) * TC + c + 1)
                        pool.tensor_tensor(xn2_s[1][:, c, :], xn2[:, c, :], xn2_s[0][:, c, :], ALU.subtract)\
                            .then_inc(xn2_lo_ready, 1)
                if second(t):
                    weight_low(4)
                if tail:
                    buf, before = slot(half, par, 2)
                    if reused(before):
                        pool.wait_ge(gated_added[buf], before * 16)
                    pool.wait_ge(gated_ready, t - 2 + 1)
                    pool.wait_ge(out_stored[buf], before * 16 + 16)
                    pool.tensor_tensor(picked_row[buf][:, :], picked_id[buf][:, :], first_row[:, :], ALU.add)\
                        .then_inc(picked_row_ready, 1)
                    pool.drain()
                    pool.indirect_dma_start(out_rows, bass.IndirectOffsetOnAxis(
                        ap=picked_row[buf][:, :].bitcast(mybir.dt.uint32), axis=0), gated[buf][:, :], None,
                        compute_op=ALU.add).then_inc(gated_added[buf], 16)
                    pool.tensor_tensor(first_row[:, :], first_row[:, :], batch_rows[:, :], ALU.add)\
                        .then_inc(picked_row_ready, 1)
                if nxt:
                    inverse_std(0, t + 1, moments1_ready, var1_ready, rstd1_ready)
                if second(t):
                    weight_low(5)
                    pool.wait_ge(w_hi_ready, NW)
                    pool.tensor_scalar(w_raw[:, 6 % W_SLOTS, :], w_raw[:, 6 % W_SLOTS, :], w_scale[:, 6:7], None,
                                       ALU.mult).then_inc(w_scaled_by_pool, 1)
                    pool.wait_ge(w_scaled_by_pool, 1)
                    weight_low(6)

            periods(pool, period)

        @block.scalar
        def _(act):
            def high(dst, src, psum_sem, count, done, scale=1.0):
                act.wait_ge(psum_sem, count)
                act.activation(dst, src, ACT.Copy, scale=scale).then_inc(done, 1)

            def weight_high(i, k0, k1):
                act.activation(w_split[i][0][:, k0:k1, :].rearrange("p k n -> p (k n)"),
                               w_raw[:, i % W_SLOTS, k0 * DIM:k1 * DIM],
                               ACT.Copy, scale=w_scale[:, i:i + 1]).then_inc(w_hi_ready, 1)

            def scale_weight(i, g):
                act.wait_ge(w_scale_ready, g + 1)
                act.activation(w_raw[:, i % W_SLOTS, :], w_raw[:, i % W_SLOTS, :], ACT.Copy,
                               scale=w_scale[:, i:i + 1]).then_inc(w_scaled_ready, 1)

            def scaled_weight_high(i):
                act.wait_ge(w_scaled_ready, max(1, i - 2))
                act.activation(w_split[i][0][:, :, :].rearrange("p k n -> p (k n)"), w_raw[:, i % W_SLOTS, :],
                               ACT.Copy).then_inc(w_hi_ready, 1)

            def gnn_qk_high(k):
                high(gnn_qk[0][:, k, :], S[k][:, :], qk_psum, k + 1, qk_hi_ready, scale=FOLD)

            act.wait_ge(w_scale_ready, 1)
            weight_high(0, 0, KC // 2)
            weight_high(0, KC // 2, KC)
            gnn_qk_high(0)
            for i in range(2):
                high(xn_t[0][0][:, 2 * i:2 * i + 2, :].rearrange("p k n -> p (k n)"), ps_xt[i][:, :],
                     xt_psum, i + 1, xt_hi_ready)
            for k in range(1, KC):
                gnn_qk_high(k)
            scale_weight(2, 1)
            scaled_weight_high(2)

            def period(t, half, par, gnn, attn, tail, nxt):
                g, a, f = t, t - 1, t - 2
                if tail:
                    for i in range(2):
                        act.wait_ge(o_psum, f * 2 + i + 1)
                        act.activation(o_cross[:, 8 * i:8 * i + 8, :],
                                       ps_o[i][:, :].rearrange("p (h s d) -> p h s d", s=2, d=DH)[:, :, 1, :],
                                       ACT.Copy).then_inc(o_cross_ready, 1)
                    high(o_t[0][:, :, :].rearrange("p k n -> p (k n)"), ps_ot[:, :], ot_psum, f + 1, ot_hi_ready)

                def xqk_high(i):
                    high(xqk_t[0][:, 2 * i:2 * i + 2, :].rearrange("p k n -> p (k n)"), ps_xqk[i][:, :],
                         xqk_psum, g * 2 + i + 1, xqk_hi_ready)

                if gnn:
                    xqk_high(0)
                if second(t):
                    act.wait_ge(w_scale_ready, 3)
                    weight_high(3, 0, KC)
                    xqk_high(1)
                if attn:
                    for c in range(TC):
                        act.wait_ge(xn2_ready, a * TC + c + 1)
                        act.activation(xn2_s[0][:, c, :], xn2[:, c, :], ACT.Copy).then_inc(xn2_hi_ready, 1)
                if second(t):
                    scale_weight(4, 2)
                    scaled_weight_high(4)
                if gnn and not second(t):
                    xqk_high(1)
                if tail:
                    buf_f, half_f = slot(half, par, 2)
                    act.wait_ge(proj_psum, f + 1)
                    if reused(half_f):
                        act.wait_ge(gated_added[buf_f], half_f * 16)
                    act.activation(gated[buf_f][:, :], ps_proj[:, :], ACT.Copy, scale=gate_out[buf_f][:, 0:1])\
                        .then_inc(gated_ready, 1)
                if attn:
                    high(sel_t[0][:, :, :].rearrange("p k n -> p (k n)"), ps_sel[0][:, :],
                         sel_psum, a * 2 + 1, sel_hi_ready)
                    act.wait_ge(picked_id_ready, a + 1)
                    act.activation(z_exp[:, :], ps_picked[:, 0:1], ACT.Exp, scale=-1.0).then_inc(z_exp_ready, 1)
                if second(t):
                    scale_weight(5, 2)
                    scaled_weight_high(5)
                if attn:
                    high(q_t[0][:, :, :].rearrange("p k n -> p (k n)"), ps_q[:, :], q_psum, a + 1, q_hi_ready)
                    high(k_t[0][:, :, :].rearrange("p k n -> p (k n)"), ps_k[:, :], k_psum, a + 1, k_hi_ready)

                def xt_high():
                    for i in range(2):
                        high(xn_t[1 - par][0][:, 2 * i:2 * i + 2, :].rearrange("p k n -> p (k n)"), ps_xt[i][:, :],
                             xt_psum, (g + 1) * 2 + i + 1, xt_hi_ready)

                if nxt and not first(t):
                    xt_high()
                if gnn:
                    act.wait_ge(al_bias_ready, g + 1)
                    for c in range(TC):
                        act.activation(al_exp[:, c, :], al_relu[:, c, :], ACT.Exp, bias=al_bias[:, c:c + 1],
                                       scale=unscale_alpha, accum_out=al_sum[:, c:c + 1]).then_inc(al_exp_ready, 1)

                def exponentials(i):
                    act.wait_ge(s_bias_ready, a * GROUPS + i + 1)
                    for j in range(KC):
                        h = 4 * i + j
                        head = GROUPS * j + i
                        last = act.activation(e[:, i, j, :], ps_scores[i][:, j * P:j * P + P], ACT.Exp,
                                              bias=s_bias[:, h:h + 1], scale=unscale_scores,
                                              accum_out=e_sum[:, head:head + 1])
                    last.then_inc(e_ready, 1)

                if second(t):
                    act.wait_ge(w_scale_ready, 4)
                    weight_high(6, 0, KC)
                if attn:
                    exponentials(0)
                    exponentials(1)
                    exponentials(2)
                    exponentials(3)
                if gnn:
                    high(y[0][:, 1, :], ps_y[1][:, :], y_psum, g * TC + 2, y1_hi_ready)
                if first(t):
                    xt_high()
                if attn:
                    for i in range(GROUPS):
                        high(e_t[0][:, i, :, :].rearrange("p k n -> p (k n)"), ps_et[i][:, :],
                             et_psum, a * GROUPS + i + 1, et_hi_ready)

            periods(act, period)

        @block.vector
        def _(dve):
            def low(dst, src, hi, hi_sem, count, done, scale=None):
                dve.wait_ge(hi_sem, count)
                if scale is None:
                    ins = dve.tensor_tensor(dst, src, hi, ALU.subtract)
                else:
                    ins = dve.scalar_tensor_tensor(out=dst, in0=src, scalar=scale, in1=hi,
                                                   op0=ALU.mult, op1=ALU.subtract)
                ins.then_inc(done, 1)

            def weight_maximum(i):
                dve.wait_ge(w_loaded[i], 16)
                dve.tensor_reduce(w_max[:, i:i + 1], w_raw[:, i % W_SLOTS, :], AX.X, ALU.max,
                                  apply_absolute_value=True).then_inc(w_max_ready, 1)

            def weight_tops(g):
                lo, up = WGROUPS[g]
                n = up - lo
                dve.wait_ge(w_top_psum, g + 1)
                dve.tensor_reduce(w_top[0:n, g:g + 1], ps_bound[g][0:n, 0:P], AX.X, ALU.max)\
                    .then_inc(w_top_ready, 1)
                dve.wait_ge(w_top_ready, g + 1)
                dve.tensor_scalar(w_diag[0:n, g, 0:n], ident[0:n, 0:n], w_top[0:n, g:g + 1], None, ALU.mult)\
                    .then_inc(w_diag_ready, 1)

            def weight_scales(g):
                lo, up = WGROUPS[g]
                n = up - lo
                dve.wait_ge(w_bound_psum, g + 1)
                dve.tensor_scalar(w_bound[:, lo:up], ps_bound[g][:, P:P + n], 1e-30, None, ALU.max)\
                    .then_inc(w_bound_ready, 1)
                dve.wait_ge(w_bound_ready, g + 1)
                dve.tensor_scalar(w_pow[:, lo:up].bitcast(i32), w_bound[:, lo:up].bitcast(i32), 0x7F800000, None,
                                  ALU.bitwise_and).then_inc(w_pow_ready, 1)
                dve.wait_ge(w_pow_ready, g + 1)
                dve.reciprocal(w_rec[:, lo:up], w_pow[:, lo:up]).then_inc(w_rec_ready, 1)
                dve.wait_ge(w_rec_ready, g + 1)
                dve.tensor_scalar(w_scale[:, lo:up], w_rec[:, lo:up], 32.0, None, ALU.mult)\
                    .then_inc(w_scale_ready, 1)

            def weight_low(i, hi_sem, count, k0=0, k1=KC):
                low(w_split[i][1][:, k0:k1, :].rearrange("p k n -> p (k n)"),
                    w_raw[:, i % W_SLOTS, k0 * DIM:k1 * DIM],
                    w_split[i][0][:, k0:k1, :].rearrange("p k n -> p (k n)"), hi_sem, count, w_lo_ready,
                    scale=w_scale[:, i:i + 1])

            def gnn_qk_low(k):
                low(gnn_qk[1][:, k, :], S[k][:, :], gnn_qk[0][:, k, :], qk_hi_ready, k + 1, qk_lo_ready, scale=FOLD)

            def statistics_of(n, c, src, stats_ready):
                dve.bn_stats(stats[n][:, c, :], src[:, c, :]).then_inc(stats_ready, 1)

            def moments_of(n, moments_ready):
                dve.drain()
                for c in range(TC):
                    dve.bn_aggr(moments[n][:, c, :], stats[n][:, c, :]).then_inc(moments_ready, 1)

            def normalise(n, dst, src, b, rstd_ready, done):
                dve.wait_ge(rstd_ready, b + 1)
                for c in range(TC):
                    dve.tensor_scalar(dst[:, c, :], src[:, c, :], moments[n][:, c, 0:1], rstd[n][:, c:c + 1],
                                      ALU.subtract, ALU.mult).then_inc(done, 1)

            def xt_low(b, buf):
                for i in range(2):
                    low(xn_t[buf][1][:, 2 * i:2 * i + 2, :].rearrange("p k n -> p (k n)"), ps_xt[i][:, :],
                        xn_t[buf][0][:, 2 * i:2 * i + 2, :].rearrange("p k n -> p (k n)"),
                        xt_hi_ready, b * 2 + i + 1, xt_lo_ready)

            dve.wait_ge(consts_ready, 5)
            weight_maximum(0)
            weight_maximum(1)
            weight_tops(0)
            weight_scales(0)
            dve.wait_ge(w_scale_ready, 1)
            for k in range(0, KC, 2):
                dve.tensor_scalar(w_split[1][0][:, k:k + 2, :].rearrange("p k n -> p (k n)"),
                                  w_raw[:, 1, k * DIM:(k + 2) * DIM],
                                  w_scale[:, 1:2], None, ALU.mult).then_inc(w1_hi_ready, 1)
            dve.scalar_tensor_tensor(out=unscale[:, 1:2], in0=w_pow[:, 0:1], scalar=1.0 / (1024.0 * FOLD),
                                     in1=w_pow[:, 1:2], op0=ALU.mult, op1=ALU.mult).then_inc(unscale_ready, 1)
            dve.wait_ge(x_loaded[0], 16)
            for c in range(TC):
                statistics_of(0, c, x_in[0], stats1_ready)
            moments_of(0, moments1_ready)
            weight_low(0, w_hi_ready, 2)
            weight_low(1, w1_hi_ready, 2)
            normalise(0, xn, x_in[0], 0, rstd1_ready, xn_ready)
            weight_maximum(2)
            weight_tops(1)
            gnn_qk_low(0)
            xt_low(0, 0)
            weight_scales(1)
            for k in range(1, KC):
                gnn_qk_low(k)
            dve.wait_ge(w_scale_ready, 2)
            dve.tensor_scalar(unscale[:, 2:3], w_pow[:, 2:3], 1.0 / 32.0, None, ALU.mult).then_inc(unscale_ready, 1)
            weight_maximum(3)

            def period(t, half, par, gnn, attn, tail, nxt):
                g, a, f = t, t - 1, t - 2
                buf_g, _ = slot(half, par, 0)
                buf_a, half_a = slot(half, par, 1)
                buf_f, _ = slot(half, par, 2)
                if attn:
                    if reused(half_a):
                        dve.wait_ge(out_stored[buf_a], half_a * 16)
                    for c in range(TC):
                        dve.wait_ge(msg_psum, a * TC + c + 1)
                        dve.scalar_tensor_tensor(out=x_mid[buf_a][:, c, :], in0=ps_msg[c][:, :], scalar=unscale_w,
                                                 in1=x_in[buf_a][:, c, :], op0=ALU.mult, op1=ALU.add)\
                            .then_inc(x_mid_ready, 1)
                if tail:
                    for i in range(2):
                        dve.wait_ge(o_cross_ready, f * 2 + i + 1)
                        dve.tensor_tensor(o_sum[:, 8 * i:8 * i + 8, :],
                                          ps_o[i][:, :].rearrange("p (h s d) -> p h s d", s=2, d=DH)[:, :, 0, :],
                                          o_cross[:, 8 * i:8 * i + 8, :], ALU.add).then_inc(o_sum_ready, 1)
                if attn:
                    dve.wait_ge(x_mid_ready, a * TC + TC)
                    for c in range(TC):
                        statistics_of(1, c, x_mid[buf_a], stats2_ready)
                    moments_of(1, moments2_ready)
                if second(t):
                    weight_scales(2)
                    dve.scalar_tensor_tensor(out=unscale[:, 4:5], in0=w_pow[:, 3:4],
                                             scalar=1.0 / (1024.0 * math.sqrt(DH)), in1=w_pow[:, 4:5],
                                             op0=ALU.mult, op1=ALU.mult).then_inc(unscale_ready, 1)
                if attn:
                    normalise(1, xn2, x_mid[buf_a], a, rstd2_ready, xn2_ready)
                    for c in range(TC):
                        dve.wait_ge(xn2_ready, a * TC + c + 1)
                        dve.scalar_tensor_tensor(out=z_junk[:, c, :], in0=xn2[:, c, :], scalar=1.0,
                                                 in1=gate_row[:, :], op0=ALU.mult, op1=ALU.mult,
                                                 accum_out=z[:, c:c + 1]).then_inc(z_ready, 1)
                if tail:
                    low(o_t[1][:, :, :].rearrange("p k n -> p (k n)"), ps_ot[:, :],
                        o_t[0][:, :, :].rearrange("p k n -> p (k n)"), ot_hi_ready, f + 1, ot_lo_ready)

                def xqk_low(i):
                    low(xqk_t[1][:, 2 * i:2 * i + 2, :].rearrange("p k n -> p (k n)"), ps_xqk[i][:, :],
                        xqk_t[0][:, 2 * i:2 * i + 2, :].rearrange("p k n -> p (k n)"),
                        xqk_hi_ready, g * 2 + i + 1, xqk_lo_ready)

                if gnn:
                    xqk_low(0)
                if second(t):
                    xqk_low(1)
                if attn:
                    dve.wait_ge(z_psum, a + 1)
                    for c in range(TC):
                        dve.scalar_tensor_tensor(out=cmp_junk[:, c, :], in0=ps_z[:, 0:TOKENS], scalar=z[:, c:c + 1],
                                                 in1=tie[:, c, :], op0=ALU.subtract, op1=ALU.is_gt,
                                                 accum_out=rank[:, c:c + 1]).then_inc(rank_ready, 1)
                    for c in range(TC):
                        dve.wait_ge(rank_ready, a * TC + c + 1)
                        dve.tensor_scalar(pick[:, c, :], rank_row[:, :], rank[:, c:c + 1], None, ALU.is_equal)\
                            .then_inc(pick_ready, 1)
                    dve.tensor_scalar(z_near[:, :], z[:, :], 60000.0, -60000.0, ALU.min, ALU.max)\
                        .then_inc(z_near_ready, 1)
                    dve.wait_ge(z_near_ready, a + 1)
                    dve.tensor_copy(z_id[:, 0, :, 0], z_near[:, :]).then_inc(z_hi_ready, 1)
                    dve.wait_ge(z_hi_ready, a + 1)
                    dve.tensor_tensor(z_id[:, 1, :, 0], z_near[:, :], z_id[:, 0, :, 0], ALU.subtract)\
                        .then_inc(z_lo_ready, 1)
                if gnn and not second(t):
                    xqk_low(1)
                if attn:
                    if second(t):
                        weight_low(3, w_hi_ready, 4)
                    dve.wait_ge(sel_psum, a * 2 + 2)
                    dve.tensor_copy(sel_t[1][:, :, :].rearrange("p k n -> p (k n)"), ps_sel[1][:, :])\
                        .then_inc(sel_lo_ready, 1)
                    dve.wait_ge(picked_psum, a + 1)
                    dve.tensor_scalar(picked_id[buf_a][:, :], ps_picked[:, 1:2], float(TOKENS - 1), None, ALU.min)\
                        .then_inc(picked_id_ready, 1)
                    dve.wait_ge(z_exp_ready, a + 1)
                    dve.tensor_scalar(z_den[:, :], z_exp[:, :], 1.0, None, ALU.add).then_inc(z_den_ready, 1)
                    dve.wait_ge(z_den_ready, a + 1)
                    dve.reciprocal(gate[:, :], z_den[:, :]).then_inc(gate_ready, 1)

                def output_gate():
                    dve.wait_ge(gate_ready, a + 1)
                    dve.tensor_scalar(gate_out[buf_a][:, :], gate[:, :], unscale_out, None, ALU.mult)\
                        .then_inc(gate_out_ready, 1)

                if attn and not second(t):
                    output_gate()
                if nxt:
                    buf_n, half_n = slot(half, par, -1)
                    dve.wait_ge(x_loaded[buf_n], half_n * 16 + 16)
                    for c in range(TC):
                        statistics_of(0, c, x_in[buf_n], stats1_ready)
                    moments_of(0, moments1_ready)
                    if first(t):
                        weight_maximum(4)
                    if second(t):
                        weight_maximum(6)
                    if not first(t):
                        normalise(0, xn, x_in[buf_n], g + 1, rstd1_ready, xn_ready)
                if attn:
                    low(q_t[1][:, :, :].rearrange("p k n -> p (k n)"), ps_q[:, :],
                        q_t[0][:, :, :].rearrange("p k n -> p (k n)"), q_hi_ready, a + 1, q_lo_ready)
                    low(k_t[1][:, :, :].rearrange("p k n -> p (k n)"), ps_k[:, :],
                        k_t[0][:, :, :].rearrange("p k n -> p (k n)"), k_hi_ready, a + 1, k_lo_ready)
                if gnn:
                    dve.wait_ge(alpha_psum, g + 1)
                    dve.wait_ge(adj_loaded[buf_g], half * 16 + 16)
                    dve.scalar_tensor_tensor(out=al_masked[:, :, :].rearrange("p c n -> p (c n)"),
                                             in0=adj_in[buf_g][:, :, :].rearrange("p c n -> p (c n)"), scalar=0.0,
                                             in1=ps_alpha[:, :], op0=ALU.not_equal, op1=ALU.mult)\
                        .then_inc(al_masked_ready, 1)
                    dve.wait_ge(al_masked_ready, g + 1)
                    for c in range(TC):
                        dve.tensor_scalar(al_relu[:, c, :], al_masked[:, c, :], 0.0, None, ALU.max, ALU.max,
                                          accum_out=al_max[:, c:c + 1]).then_inc(al_relu_ready, 1)
                    dve.wait_ge(al_relu_ready, g * TC + TC)
                    dve.tensor_scalar(al_bias[:, :], al_max[:, :], unscale_alpha, -1.0, ALU.mult, ALU.mult)\
                        .then_inc(al_bias_ready, 1)
                if first(t):
                    normalise(0, xn, x_in[buf_n], g + 1, rstd1_ready, xn_ready)
                if second(t):
                    weight_tops(3)
                if nxt and not first(t):
                    xt_low(g + 1, 1 - par)
                if second(t):
                    weight_scales(3)
                    dve.scalar_tensor_tensor(out=unscale[:, 6:7], in0=w_pow[:, 5:6], scalar=1.0 / 1024.0,
                                             in1=w_pow[:, 6:7], op0=ALU.mult, op1=ALU.mult).then_inc(unscale_ready, 1)
                    dve.wait_ge(unscale_ready, 4)
                    output_gate()
                if attn:
                    dve.wait_ge(scores_psum, a + 1)
                    for i in range(GROUPS):
                        dve.tensor_reduce(s_max[:, 4 * i:4 * i + 4],
                                          ps_scores[i][:, :].rearrange("p (j n) -> p j n", n=P), AX.X, ALU.max)\
                            .then_inc(s_max_ready, 1)
                        dve.wait_ge(s_max_ready, a * GROUPS + i + 1)
                        dve.tensor_scalar(s_bias[:, 4 * i:4 * i + 4], s_max[:, 4 * i:4 * i + 4], unscale_scores, -1.0,
                                          ALU.mult, ALU.mult).then_inc(s_bias_ready, 1)

                def split_y0():
                    dve.wait_ge(y_psum, g * TC + 1)
                    dve.tensor_copy(y[0][:, 0, :], ps_y[0][:, :]).then_inc(y0_hi_ready, 1)
                    low(y[1][:, 0, :], ps_y[0][:, :], y[0][:, 0, :], y0_hi_ready, g + 1, y_lo_ready)

                if first(t):
                    split_y0()
                if gnn:
                    dve.wait_ge(al_exp_ready, g * TC + TC)
                    dve.reciprocal(al_rec[:, :], al_sum[:, :]).then_inc(al_rec_ready, 1)
                    dve.wait_ge(al_rec_ready, g + 1)
                    for c in range(TC):
                        dve.tensor_scalar(alpha[0][:, c, :], al_exp[:, c, :], al_rec[:, c:c + 1], None, ALU.mult)\
                            .then_inc(alpha_hi_ready, 1)
                    for c in range(TC):
                        low(alpha[1][:, c, :], al_exp[:, c, :], alpha[0][:, c, :], alpha_hi_ready,
                            g * TC + c + 1, alpha_lo_ready, scale=al_rec[:, c:c + 1])
                if attn:
                    dve.wait_ge(v_psum, a + 1)
                    dve.tensor_copy(v[:, :, 0, :], ps_v[:, :].rearrange("p (h d) -> p h d", d=DH))\
                        .then_inc(v_hi_ready, 1)
                    low(v[:, :, 1, :], ps_v[:, :].rearrange("p (h d) -> p h d", d=DH), v[:, :, 0, :],
                        v_hi_ready, a + 1, v_lo_ready)
                if gnn:
                    if not first(t):
                        split_y0()
                    low(y[1][:, 1, :], ps_y[1][:, :], y[0][:, 1, :], y1_hi_ready, g + 1, y_lo_ready)
                if first(t):
                    xt_low(g + 1, 1 - par)
                    weight_maximum(5)
                    weight_tops(2)
                if attn:
                    dve.wait_ge(e_ready, a * GROUPS + GROUPS)
                    dve.reciprocal(o_rec[:, :], e_sum[:, :]).then_inc(o_rec_ready, 1)
                    for i in range(GROUPS):
                        low(e_t[1][:, i, :, :].rearrange("p k n -> p (k n)"), ps_et[i][:, :],
                            e_t[0][:, i, :, :].rearrange("p k n -> p (k n)"), et_hi_ready,
                            a * GROUPS + i + 1, et_lo_ready)

            dve.wait_ge(unscale_ready, 2)
            dve.wait_ge(gate_row_loaded, 16)
            periods(dve, period)

        @block.tensor
        def _(pe):
            PASSES = ((0, 0), (0, 1), (1, 0))

            def product(dst, steps, lhs, rhs, passes=range(3)):
                for n in passes:
                    l, r = PASSES[n]
                    for k in range(steps):
                        last = pe.matmul(dst, lhs(l, k), rhs(r, k), start=(n == 0 and k == 0),
                                         stop=(n == 2 and k == steps - 1))
                return last

            def weight_rows(g):
                lo, up = WGROUPS[g]
                pe.transpose(ps_bound[g][0:up - lo, 0:P], w_max[:, lo:up], ident[:, :]).then_inc(w_top_psum, 1)

            def weight_bounds(g):
                lo, up = WGROUPS[g]
                n = up - lo
                pe.wait_ge(w_diag_ready, g + 1)
                pe.matmul(ps_bound[g][:, P:P + n], ones[0:n, :], w_diag[0:n, g, 0:n], start=True, stop=True)\
                    .then_inc(w_bound_psum, 1)

            def transpose_x(b):
                pe.wait_ge(xn_ready, b * TC + TC)
                for i in range(2):
                    for k in (2 * i, 2 * i + 1):
                        for c in range(TC):
                            at = (k % 2) * TOKENS + c * P
                            last = pe.transpose(ps_xt[i][:, at:at + P], xn[:, c, k * P:k * P + P], ident[:, :])
                    last.then_inc(xt_psum, 1)

            pe.wait_ge(consts_ready, 5)
            pe.wait_ge(w_max_ready, 2)
            weight_rows(0)
            weight_bounds(0)

            def gnn_qk_product(k, passes):
                return product(S[k][:, :], KC, lambda p, o: w_split[0][p][:, o, k * P:k * P + P],
                               lambda p, o: w_split[1][p][:, o, :], passes)

            for o in range(KC):
                pe.wait_ge(w_hi_ready, o // 2 + 1)
                pe.wait_ge(w1_hi_ready, o // 2 + 1)
                for k in range(KC):
                    pe.matmul(S[k][:, :], w_split[0][0][:, o, k * P:k * P + P], w_split[1][0][:, o, :],
                              start=(o == 0), stop=False)
            pe.wait_ge(w_lo_ready, 2)
            for k in range(KC):
                gnn_qk_product(k, range(1, 3)).then_inc(qk_psum, 1)
                if k == 0:
                    transpose_x(0)
                    pe.wait_ge(w_max_ready, 3)
                    weight_rows(1)
                if k == 1:
                    weight_bounds(1)
            pe.wait_ge(qk_hi_ready, KC)
            pe.wait_ge(qk_lo_ready, 1)

            def head_scores(tiles, groups):
                for j in tiles:
                    for n, (l, r) in enumerate(PASSES):
                        for i in groups:
                            rows = slice(i * DH, i * DH + DH)
                            last = pe.matmul(ps_scores[i][:, j * P:j * P + P], q_t[l][rows, j, :], k_t[r][rows, j, :],
                                             start=(n == 0), stop=(n == 2))
                return last

            def project(passes):
                return product(ps_proj[:, :], KC, lambda p, k: o_t[p][:, k, :],
                               lambda p, k: w_split[6][p][:, k, :], passes)

            def period(t, half, par, gnn, attn, tail, nxt):
                g, a, f = t, t - 1, t - 2
                x_t = xn_t[par]

                def xqk(j, passes=range(3)):
                    return product(ps_xqk[j // 2][:, (j % 2) * TOKENS:(j % 2 + 1) * TOKENS], KC,
                                   lambda p, k: gnn_qk[p][:, k, j * P:j * P + P], lambda p, k: x_t[p][:, k, :],
                                   passes)

                def scores_t(m):
                    return product(ps_alpha[:, m * TOKENS:(m + 1) * TOKENS], KC,
                                   lambda p, k: x_t[p][:, k, m * P:m * P + P], lambda p, k: xqk_t[p][:, k, :])

                if gnn:
                    pe.wait_ge(xt_lo_ready, g * 2 + 2)
                    if first(t):
                        xqk(0, range(2))
                        pe.wait_ge(qk_lo_ready, KC)
                        xqk(0, (2,))
                    else:
                        xqk(0)
                    if second(t):
                        weight_bounds(2)
                if gnn:
                    xqk(1, range(2))
                if tail:
                    pe.wait_ge(o_norm_ready, f * 2 + 2)
                    for k in range(KC):
                        last = pe.transpose(ps_ot[:, k * P:k * P + P],
                                            o_norm[:, :, :].rearrange("p h d -> p (h d)")[:, k * P:k * P + P],
                                            ident[:, :])
                    last.then_inc(ot_psum, 1)
                if gnn:
                    xqk(1, (2,)).then_inc(xqk_psum, 1)
                    xqk(2)
                if tail:
                    pe.wait_ge(ot_hi_ready, f + 1)
                    project(range(2))
                if second(t):
                    xqk(3).then_inc(xqk_psum, 1)
                if attn:
                    pe.wait_ge(z_ready, a * TC + TC)
                    for c in range(TC):
                        last = pe.transpose(ps_z[:, c * P:c * P + P], z[:, c:c + 1].to_broadcast([P, P]), ident[:, :])
                    last.then_inc(z_psum, 1)
                if gnn and not second(t):
                    xqk(3).then_inc(xqk_psum, 1)
                if tail:
                    pe.wait_ge(ot_lo_ready, f + 1)
                    project((2,)).then_inc(proj_psum, 1)
                if second(t):
                    pe.wait_ge(xqk_lo_ready, g * 2 + 2)
                    scores_t(0)

                def pick_part(p):
                    for k in range(KC):
                        for c in range(TC):
                            last = pe.matmul(ps_sel[p][:, k * P:k * P + P], xn2_s[p][:, c, k * P:k * P + P],
                                             pick[:, c, :], start=(c == 0), stop=(c == TC - 1))
                    last.then_inc(sel_psum, 1)

                if attn:
                    pe.wait_ge(pick_ready, a * TC + TC)
                    pe.wait_ge(xn2_hi_ready, a * TC + TC)
                    pick_part(0)
                    pe.wait_ge(xn2_lo_ready, a * TC + TC)
                    pick_part(1)
                    pe.wait_ge(z_lo_ready, a + 1)
                    for c in range(TC):
                        for p in range(2):
                            last = pe.matmul(ps_picked, pick[:, c, :], z_id[:, p, c, :], start=(c == 0 and p == 0),
                                             stop=(c == TC - 1 and p == 1))
                    last.then_inc(picked_psum, 1)
                if tail:
                    pe.wait_ge(gated_ready, f + 1)
                if gnn and not second(t):
                    pe.wait_ge(xqk_lo_ready, g * 2 + 2)
                    scores_t(0)
                if second(t):
                    scores_t(1).then_inc(alpha_psum, 1)
                if attn:
                    pe.wait_ge(sel_hi_ready, a + 1)
                    pe.wait_ge(sel_lo_ready, a + 1)
                    for w, ps, done in ((3, ps_q, q_psum), (4, ps_k, k_psum)):
                        if second(t) and w == 3:
                            pe.wait_ge(w_lo_ready, 3)
                        if second(t) and w == 4:
                            pe.wait_ge(w_low_by_pool, 2)
                        for j in range(KC):
                            last = product(ps[:, j * P:j * P + P], KC,
                                           lambda p, k: w_split[w][p][:, k, j * P:j * P + P],
                                           lambda p, k: sel_t[p][:, k, :])
                        last.then_inc(done, 1)
                if gnn and not second(t):
                    scores_t(1).then_inc(alpha_psum, 1)
                if nxt and not first(t):
                    transpose_x(g + 1)
                if attn:
                    pe.wait_ge(q_lo_ready, a + 1)
                    pe.wait_ge(k_lo_ready, a + 1)
                    pe.wait_ge(z_exp_ready, a + 1)
                    if second(t):
                        pe.wait_ge(w_max_ready, NW)
                        weight_rows(3)
                    head_scores(range(2), range(GROUPS - 1))
                    if gnn:
                        pe.wait_ge(al_masked_ready, g + 1)
                    head_scores(range(2), (GROUPS - 1,))
                    last = head_scores(range(2, KC), range(GROUPS))
                    last.then_inc(scores_psum, 1)
                    if second(t):
                        weight_bounds(3)
                    if nxt:
                        pe.wait_ge(xt_lo_ready, (g + 1) * 2 + 1)
                    if second(t):
                        pe.wait_ge(w_low_by_pool, 3)
                    product(ps_v[:, :], KC, lambda p, k: sel_t[p][:, k, :], lambda p, k: w_split[5][p][:, k, :])\
                        .then_inc(v_psum, 1)
                if gnn:
                    if second(t):
                        pe.wait_ge(w_bound_ready, 4)
                    if first(t):
                        pe.wait_ge(w_low_by_pool, 1)
                    if nxt and not first(t):
                        pe.wait_ge(xt_lo_ready, (g + 1) * 2 + 2)
                    for m in range(TC):
                        product(ps_y[m][:, :], KC, lambda p, k: x_t[p][:, k, m * P:m * P + P],
                                lambda p, k: w_split[2][p][:, k, :]).then_inc(y_psum, 1)
                    if first(t):
                        pe.wait_ge(y_lo_ready, 1)
                        transpose_x(g + 1)
                if attn:
                    for i in range(GROUPS):
                        pe.wait_ge(e_ready, a * GROUPS + i + 1)
                        for j in range(KC):
                            last = pe.transpose(ps_et[i][:, j * P:j * P + P], e[:, i, j, :], ident[:, :])
                        last.then_inc(et_psum, 1)
                if gnn:
                    pe.wait_ge(y_lo_ready, g * TC + TC)
                    pe.wait_ge(alpha_lo_ready, g * TC + TC)
                    if first(t):
                        pe.wait_ge(xt_lo_ready, (g + 1) * 2 + 2)
                    for c in range(TC):
                        product(ps_msg[c][:, :], TC, lambda p, m: alpha[p][:, m, c * P:c * P + P],
                                lambda p, m: y[p][:, m, :]).then_inc(msg_psum, 1)
                if first(t):
                    pe.wait_ge(w_max_ready, 6)
                    weight_rows(2)
                if attn:
                    pe.wait_ge(et_lo_ready, a * GROUPS + GROUPS)
                    pe.wait_ge(v_lo_ready, a + 1)
                    for i in range(2):
                        for h in range(8 * i, 8 * i + 8):
                            at = (h - 8 * i) * 2 * DH
                            pe.matmul(ps_o[i][:, at:at + 2 * DH], e_t[0][:, h % GROUPS, h // GROUPS, :],
                                      v[:, h, :, :].rearrange("p s d -> p (s d)"), start=True, stop=False)
                            last = pe.matmul(ps_o[i][:, at:at + DH], e_t[1][:, h % GROUPS, h // GROUPS, :],
                                             v[:, h, 0, :], start=False, stop=True)
                        last.then_inc(o_psum, 1)
                if second(t):
                    pe.wait_ge(w_low_by_pool, 4)

            periods(pe, period)


_NAMES = ["x", "adj_t", "gnn_w", "gnn_wq_t", "gnn_wk_t", "gate_w", "wq", "wk", "wv", "wo"]


def kernel(x, adj, L0_gnn_weight, L0_gnn_wq, L0_gnn_wk, L0_ffn_Wg, L0_ffn_Wq, L0_ffn_Wk, L0_ffn_Wv, L0_ffn_Wo):
    import numpy as _np
    import concourse.bacc as _bacc
    from concourse import mybir as _mybir
    from concourse.bass_utils import run_bass_kernel_spmd as _run

    given = [
        _np.asarray(x), _np.asarray(adj).transpose(0, 2, 1), _np.asarray(L0_gnn_weight),
        _np.asarray(L0_gnn_wq).T, _np.asarray(L0_gnn_wk).T, _np.asarray(L0_ffn_Wg).reshape(-1),
        _np.asarray(L0_ffn_Wq), _np.asarray(L0_ffn_Wk), _np.asarray(L0_ffn_Wv), _np.asarray(L0_ffn_Wo),
    ]
    nc = _bacc.Bacc("TRN2", target_bir_lowering=False, num_devices=1)
    arrays, args = {}, []
    for name, a in zip(_NAMES, given):
        a = _np.ascontiguousarray(a)
        arrays[f"in_{name}"] = a
        args.append(nc.dram_tensor(f"in_{name}", a.shape, _mybir.dt.from_np(a.dtype), kind="ExternalInput").ap())
    args.append(nc.dram_tensor("out_0", given[0].shape, _mybir.dt.float32, kind="ExternalOutput").ap())
    gnn_then_routed_attention(nc, *args)
    result = _run(nc, [arrays], core_ids=[0])
    return result.results[0]["out_0"]
```
